# Optimizing a Trainium2 kernel written in Bass

```python
import numpy as np
import jax
import jax.numpy as jnp

def _softmax(x, axis=-1):
    return jax.nn.softmax(x, axis=axis)

def _gelu(x):
    return jax.nn.gelu(x, approximate=True)

def _silu(x):
    return jax.nn.silu(x)

def _sigmoid(x):
    return jax.nn.sigmoid(x)

def _layernorm(x, axis=-1, eps=1e-05):
    m = jnp.mean(x, axis=axis, keepdims=True)
    v = jnp.var(x, axis=axis, keepdims=True)
    return (x - m) / jnp.sqrt(v + eps)

def _scatter_add(tgt, idx, src, axis=0):
    return tgt.at[idx].add(src)

def _segment_sum(src, seg, n):
    return jax.ops.segment_sum(src, seg, n)
kernel_name = 'mk_perceiver_d2_seqx_r8_9b854c'

def setup_inputs(seed: int=0):
    np.random.seed(seed)
    _w = jnp.asarray

    def _rec_inputs():
        import jax
        import jax.numpy as jnp
        _rk = jax.random.key(seed)
        x = -0.0002928 + 1 * jax.random.normal(jax.random.fold_in(_rk, 1), (128, 32, 128), jnp.float32)
        _lenS = 32 - jax.random.randint(jax.random.fold_in(_rk, 7), (128,), 0, max(1, 32 // 4) + 1, jnp.int32)
        _lenS2 = 257 - jax.random.randint(jax.random.fold_in(_rk, 8), (128,), 0, max(1, 257 // 4) + 1, jnp.int32)
        _ctx_1024P = jax.random.normal(jax.random.fold_in(_rk, 11), (128, 16, 128), jnp.float32)
        _ctx_1024c = jax.random.dirichlet(jax.random.fold_in(_rk, 511), 0.3 * jnp.ones((16,), jnp.float32), (128, 257))
        _ctx_1024t = jnp.einsum('bsk,bkd->bsd', _ctx_1024c, _ctx_1024P)
        _ctx_1024t = _ctx_1024t * jax.lax.rsqrt(jnp.mean(jnp.square(_ctx_1024t)) + 1e-12) * 0.953939
        ctx_1024 = -1.78809e-06 + 0.0312453 * (_ctx_1024t + 0.3 * jax.random.normal(jax.random.fold_in(_rk, 611), (128, 257, 128), jnp.float32))
        _validS = jnp.arange(32)[None, :] < _lenS[:, None]
        _validS2 = jnp.arange(257)[None, :] < _lenS2[:, None]
        _causal = jnp.tril(jnp.ones((32, 32), dtype=bool))
        mask_1x1xSxS2_fk0 = jnp.where(jnp.broadcast_to(_validS2[0:1, None, None, :], (1, 1, 32, 257)), -1000000000.0, 0.0).astype(jnp.float32)
        mask_BxS2_bk0 = jnp.logical_not(jnp.broadcast_to(_validS2[:, :], (128, 257)))
        return (x, ctx_1024, mask_1x1xSxS2_fk0, mask_BxS2_bk0)
    x, ctx_1024, mask_1x1xSxS2_fk0, mask_BxS2_bk0 = _rec_inputs()

    def _L0_xattn_setup():
        import jax, jax.numpy as jnp
        import numpy as np
        E, TPE, H, F = (64, 64, 128, 128)
        key = jax.random.key(seed)
        k1, k2, k3, k4 = jax.random.split(key, 4)
        scale = 1.0 / np.sqrt(H)
        return {'x': jax.random.normal(k1, (E, TPE, H), dtype=jnp.float32), 'w1': jax.random.normal(k2, (E, F, H), dtype=jnp.float32) * scale, 'v1': jax.random.normal(k3, (E, F, H), dtype=jnp.float32) * scale, 'w2': jax.random.normal(k4, (E, F, H), dtype=jnp.float32) * scale}
    _L0_xattn_all = _L0_xattn_setup()
    _L0_xattn_in = {k: v for k, v in _L0_xattn_all.items() if k in ()}
    del _L0_xattn_all

    def _L0_attn_setup():
        import jax, jax.numpy as jnp
        import numpy as np
        B, N, D_MODEL = (4, 512, 128)
        HEADS, DIM_HEAD = (16, 64)
        HIDDEN = HEADS * DIM_HEAD
        SCALE = DIM_HEAD ** (-0.5)
        key = jax.random.key(seed)
        k1, k2, k3, k4 = jax.random.split(key, 4)
        x = jax.random.normal(k1, (B, N, D_MODEL), dtype=jnp.float32)
        w_qkv = jax.random.normal(k2, (D_MODEL, 3 * HIDDEN), dtype=jnp.float32) * D_MODEL ** (-0.5)
        w_out = jax.random.normal(k3, (HIDDEN, D_MODEL), dtype=jnp.float32) * HIDDEN ** (-0.5)
        b_out = jax.random.normal(k4, (D_MODEL,), dtype=jnp.float32) * 0.01
        return {'x': x, 'w_qkv': w_qkv, 'w_out': w_out, 'b_out': b_out}
    _L0_attn_all = _L0_attn_setup()
    _L0_attn_in = {k: v for k, v in _L0_attn_all.items() if k in ('w_qkv', 'w_out', 'b_out')}
    del _L0_attn_all

    def _L0_ffn_setup():
        import jax, jax.numpy as jnp
        import numpy as np
        NH, NKV, E, K = (16, 4, 8, 2)
        CAP_FACTOR = 1.25
        LN_EPS = 1e-05

        def _layer_norm(x, w, b):
            mu = jnp.mean(x, axis=-1, keepdims=True)
            var = jnp.mean(jnp.square(x - mu), axis=-1, keepdims=True)
            return (x - mu) * jax.lax.rsqrt(var + LN_EPS) * w + b
        key = jax.random.key(seed)
        ks = jax.random.split(key, 6)
        S, B, H, F = (256, 1, 128, 256)
        HD = H // NH
        qkv_out = NKV * (NH // NKV + 2) * HD
        f32 = jnp.float32
        return {'hidden_states': jax.random.normal(ks[0], (S, B, H), f32), 'ln1_weight': jnp.ones((H,), f32), 'ln1_bias': jnp.zeros((H,), f32), 'ln2_weight': jnp.ones((H,), f32), 'ln2_bias': jnp.zeros((H,), f32), 'qkv_weight': jax.random.normal(ks[1], (qkv_out, H), f32) * 0.02, 'proj_weight': jax.random.normal(ks[2], (H, H), f32) * 0.02, 'router_weight': jax.random.normal(ks[3], (H, E), f32) * 0.02, 'moe_w1': jax.random.normal(ks[4], (E, H, F), f32) * 0.02, 'moe_w2': jax.random.normal(ks[5], (F and E, F, H), f32)[:E] * 0.02 if False else jax.random.normal(ks[5], (E, F, H), f32) * 0.02}
    _L0_ffn_all = _L0_ffn_setup()
    _L0_ffn_in = {k: v for k, v in _L0_ffn_all.items() if k in ('ln1_weight', 'ln1_bias', 'ln2_weight', 'ln2_bias', 'qkv_weight', 'proj_weight', 'router_weight', 'moe_w1', 'moe_w2')}
    del _L0_ffn_all

    def _L1_xattn_setup():
        import jax, jax.numpy as jnp
        import numpy as np
        D_MODEL = 128
        N_HEADS = 16
        HEAD_DIM = D_MODEL // N_HEADS
        ROPE_BASE = 10000.0
        NEG_INF = -1000000000.0

        def rotate_half(x):
            x1 = x[..., ::2]
            x2 = x[..., 1::2]
            return jnp.stack((-x2, x1), axis=-1).reshape(x.shape)

        def rope_sin_cos(seq_len, head_dim, dtype):
            inv_freq = 1.0 / ROPE_BASE ** (jnp.arange(0, head_dim, 2, dtype=jnp.float32) / head_dim)
            t = jnp.arange(seq_len, dtype=jnp.float32)
            freqs = jnp.einsum('i,j->ij', t, inv_freq)
            emb = jnp.concatenate((freqs, freqs), axis=-1)
            return (jnp.sin(emb).astype(dtype), jnp.cos(emb).astype(dtype))

        def apply_rope(x, sin, cos):
            return x * cos[None, None] + rotate_half(x) * sin[None, None]
        key = jax.random.key(seed)
        ks = jax.random.split(key, 9)
        B, T, D = (2, 256, D_MODEL)
        q = jax.random.normal(ks[0], (B, T, D), dtype=jnp.float32)
        k = jax.random.normal(ks[1], (B, T, D), dtype=jnp.float32)
        v = jax.random.normal(ks[2], (B, T, D), dtype=jnp.float32)
        causal = jnp.triu(jnp.full((T, T), NEG_INF, dtype=jnp.float32), k=1)
        attn_mask = causal[None, None]
        key_padding_mask = jax.random.uniform(ks[3], (B, T)) < 0.05
        scale = 1.0 / np.sqrt(D)
        Wq = jax.random.normal(ks[4], (D, D), dtype=jnp.float32) * scale
        Wk = jax.random.normal(ks[5], (D, D), dtype=jnp.float32) * scale
        Wv = jax.random.normal(ks[6], (D, D), dtype=jnp.float32) * scale
        Wo = jax.random.normal(ks[7], (D, D), dtype=jnp.float32) * scale
        return {'q': q, 'k': k, 'v': v, 'attn_mask': attn_mask, 'key_padding_mask': key_padding_mask, 'Wq': Wq, 'Wk': Wk, 'Wv': Wv, 'Wo': Wo}
    _L1_xattn_all = _L1_xattn_setup()
    _L1_xattn_in = {k: v for k, v in _L1_xattn_all.items() if k in ('Wq', 'Wk', 'Wv', 'Wo')}
    del _L1_xattn_all

    def _L1_attn_setup():
        import jax, jax.numpy as jnp
        import numpy as np
        B, N, D = (2, 256, 128)
        H, QH, DH = (8, 16, 64)
        SOFTCLAMP = 50.0

        def _rmsnorm(x, w):
            eps = jnp.finfo(x.dtype).eps
            return x * jax.lax.rsqrt(jnp.mean(x * x, axis=-1, keepdims=True) + eps) * w

        def _l2norm(x):
            n = jnp.maximum(jnp.linalg.norm(x, axis=-1, keepdims=True), 1e-12)
            return x / n

        def _mh_rmsnorm(x, gamma):
            scale = (gamma + 1.0) * np.sqrt(x.shape[-1]).astype(np.float32)
            return _l2norm(x) * scale[None, :, None, :]
        key = jax.random.key(seed)
        ks = jax.random.split(key, 7)
        return {'tokens': jax.random.normal(ks[0], (B, N, D), jnp.float32), 'norm_w': jnp.ones((D,), jnp.float32) + 0.02 * jax.random.normal(ks[1], (D,), jnp.float32), 'Wq': 0.02 * jax.random.normal(ks[2], (D, QH * DH), jnp.float32), 'Wkv': 0.02 * jax.random.normal(ks[3], (D, 2 * H * DH), jnp.float32), 'Wout': 0.02 * jax.random.normal(ks[4], (H * DH, D), jnp.float32), 'q_gamma': 0.02 * jax.random.normal(ks[5], (QH, DH), jnp.float32), 'k_gamma': 0.02 * jax.random.normal(ks[6], (H, DH), jnp.float32)}
    _L1_attn_all = _L1_attn_setup()
    _L1_attn_in = {k: v for k, v in _L1_attn_all.items() if k in ('norm_w', 'Wq', 'Wkv', 'Wout', 'q_gamma', 'k_gamma')}
    del _L1_attn_all

    def _L1_ffn_setup():
        import jax, jax.numpy as jnp
        import numpy as np
        HIDDEN = 128
        INTER = 512
        N_EXPERTS = 8

        def geglu(x, w1, w2, w3):
            return jax.nn.gelu(x @ w1, approximate=False) * (x @ w2) @ w3
        key = jax.random.key(seed)
        ks = jax.random.split(key, 8)
        s = 0.02
        x = jax.random.normal(ks[0], (2, 256, HIDDEN), dtype=jnp.float32)
        w1s = jax.random.normal(ks[1], (HIDDEN, INTER), dtype=jnp.float32) * s
        w2s = jax.random.normal(ks[2], (HIDDEN, INTER), dtype=jnp.float32) * s
        w3s = jax.random.normal(ks[3], (INTER, HIDDEN), dtype=jnp.float32) * s
        W1 = jax.random.normal(ks[4], (N_EXPERTS, HIDDEN, INTER), dtype=jnp.float32) * s
        W2 = jax.random.normal(ks[5], (N_EXPERTS, HIDDEN, INTER), dtype=jnp.float32) * s
        W3 = jax.random.normal(ks[6], (N_EXPERTS, INTER, HIDDEN), dtype=jnp.float32) * s
        Wg = jax.random.normal(ks[7], (HIDDEN, N_EXPERTS), dtype=jnp.float32) * s
        return {'x': x, 'w1s': w1s, 'w2s': w2s, 'w3s': w3s, 'W1': W1, 'W2': W2, 'W3': W3, 'Wg': Wg}
    _L1_ffn_all = _L1_ffn_setup()
    _L1_ffn_in = {k: v for k, v in _L1_ffn_all.items() if k in ('w1s', 'w2s', 'w3s', 'W1', 'W2', 'W3', 'Wg')}
    del _L1_ffn_all
    return {'x': x, 'ctx_1024': ctx_1024, 'mask_1x1xSxS2_fk0': mask_1x1xSxS2_fk0, 'mask_BxS2_bk0': mask_BxS2_bk0, 'L0_attn_w_qkv': _L0_attn_in['w_qkv'], 'L0_attn_w_out': _L0_attn_in['w_out'], 'L0_attn_b_out': _L0_attn_in['b_out'], 'L0_ffn_ln1_weight': _L0_ffn_in['ln1_weight'], 'L0_ffn_ln1_bias': _L0_ffn_in['ln1_bias'], 'L0_ffn_ln2_weight': _L0_ffn_in['ln2_weight'], 'L0_ffn_ln2_bias': _L0_ffn_in['ln2_bias'], 'L0_ffn_qkv_weight': _L0_ffn_in['qkv_weight'], 'L0_ffn_proj_weight': _L0_ffn_in['proj_weight'], 'L0_ffn_router_weight': _L0_ffn_in['router_weight'], 'L0_ffn_moe_w1': _L0_ffn_in['moe_w1'], 'L0_ffn_moe_w2': _L0_ffn_in['moe_w2'], 'L1_xattn_Wq': _L1_xattn_in['Wq'], 'L1_xattn_Wk': _L1_xattn_in['Wk'], 'L1_xattn_Wv': _L1_xattn_in['Wv'], 'L1_xattn_Wo': _L1_xattn_in['Wo'], 'L1_attn_norm_w': _L1_attn_in['norm_w'], 'L1_attn_Wq': _L1_attn_in['Wq'], 'L1_attn_Wkv': _L1_attn_in['Wkv'], 'L1_attn_Wout': _L1_attn_in['Wout'], 'L1_attn_q_gamma': _L1_attn_in['q_gamma'], 'L1_attn_k_gamma': _L1_attn_in['k_gamma'], 'L1_ffn_w1s': _L1_ffn_in['w1s'], 'L1_ffn_w2s': _L1_ffn_in['w2s'], 'L1_ffn_w3s': _L1_ffn_in['w3s'], 'L1_ffn_W1': _L1_ffn_in['W1'], 'L1_ffn_W2': _L1_ffn_in['W2'], 'L1_ffn_W3': _L1_ffn_in['W3'], 'L1_ffn_Wg': _L1_ffn_in['Wg']}

def reference(x, ctx_1024, mask_1x1xSxS2_fk0, mask_BxS2_bk0, L0_attn_w_qkv, L0_attn_w_out, L0_attn_b_out, L0_ffn_ln1_weight, L0_ffn_ln1_bias, L0_ffn_ln2_weight, L0_ffn_ln2_bias, L0_ffn_qkv_weight, L0_ffn_proj_weight, L0_ffn_router_weight, L0_ffn_moe_w1, L0_ffn_moe_w2, L1_xattn_Wq, L1_xattn_Wk, L1_xattn_Wv, L1_xattn_Wo, L1_attn_norm_w, L1_attn_Wq, L1_attn_Wkv, L1_attn_Wout, L1_attn_q_gamma, L1_attn_k_gamma, L1_ffn_w1s, L1_ffn_w2s, L1_ffn_w3s, L1_ffn_W1, L1_ffn_W2, L1_ffn_W3, L1_ffn_Wg):
    import jax
    import jax.numpy as jnp

    def _L0_xattn_ref(x, w1, v1, w2):
        import jax, jax.numpy as jnp
        import numpy as np
        E, TPE, H, F = (64, 64, 128, 128)
        h1 = jnp.einsum('eth,efh->etf', x, w1)
        h2 = jnp.einsum('eth,efh->etf', x, v1)
        g = jax.nn.gelu(h1, approximate=False) * h2
        return jnp.einsum('etf,efh->eth', g, w2)

    def _L0_attn_ref(x, w_qkv, w_out, b_out):
        import jax, jax.numpy as jnp
        import numpy as np
        B, N, D_MODEL = (4, 512, 128)
        HEADS, DIM_HEAD = (16, 64)
        HIDDEN = HEADS * DIM_HEAD
        SCALE = DIM_HEAD ** (-0.5)
        b, n, _ = x.shape
        qkv = x @ w_qkv
        q, k, v = jnp.split(qkv, 3, axis=-1)

        def to_bhdn(t):
            return t.reshape(b, n, HEADS, DIM_HEAD).transpose(0, 2, 3, 1)
        q, k, v = map(to_bhdn, (q, k, v))
        q = jax.nn.softmax(q, axis=-2) * SCALE
        k = jax.nn.softmax(k, axis=-1)
        context = jnp.einsum('bhdn,bhen->bhde', k, v)
        out = jnp.einsum('bhde,bhdn->bhen', context, q)
        out = out.transpose(0, 3, 1, 2).reshape(b, n, HIDDEN)
        return out @ w_out + b_out

    def _L0_ffn_ref(hidden_states, ln1_weight, ln1_bias, ln2_weight, ln2_bias, qkv_weight, proj_weight, router_weight, moe_w1, moe_w2):
        import jax, jax.numpy as jnp
        import numpy as np
        NH, NKV, E, K = (16, 4, 8, 2)
        CAP_FACTOR = 1.25
        LN_EPS = 1e-05

        def _layer_norm(x, w, b):
            mu = jnp.mean(x, axis=-1, keepdims=True)
            var = jnp.mean(jnp.square(x - mu), axis=-1, keepdims=True)
            return (x - mu) * jax.lax.rsqrt(var + LN_EPS) * w + b
        S, B, H = hidden_states.shape
        HD = H // NH
        q_per_kv = NH // NKV
        ln1 = _layer_norm(hidden_states, ln1_weight, ln1_bias)
        qkv = jnp.einsum('sbh,oh->sbo', ln1, qkv_weight)
        qkv = qkv.reshape(S, B, NKV, (q_per_kv + 2) * HD)
        q = qkv[..., :q_per_kv * HD].reshape(S, B, NH, HD)
        k = qkv[..., q_per_kv * HD:(q_per_kv + 1) * HD]
        v = qkv[..., (q_per_kv + 1) * HD:]
        qb = jnp.transpose(q, (1, 2, 0, 3)).reshape(B, NKV, q_per_kv, S, HD)
        kb = jnp.transpose(k, (1, 2, 0, 3))
        vb = jnp.transpose(v, (1, 2, 0, 3))
        scale = 1.0 / np.sqrt(HD).astype(np.float32)
        scores = jnp.einsum('bgqsd,bgtd->bgqst', qb, kb) * scale
        causal = jnp.tril(jnp.ones((S, S), bool))
        scores = jnp.where(causal, scores, jnp.finfo(scores.dtype).min)
        attn = jax.nn.softmax(scores, axis=-1)
        ao = jnp.einsum('bgqst,bgtd->bgqsd', attn, vb)
        ao = ao.reshape(B, NH, S, HD)
        ao = jnp.transpose(ao, (2, 0, 1, 3)).reshape(S, B, H)
        proj = jnp.einsum('sbh,oh->sbo', ao, proj_weight)
        h1 = hidden_states + proj
        ln2 = _layer_norm(h1, ln2_weight, ln2_bias)
        x = ln2.reshape(-1, H)
        N = x.shape[0]
        logits = x @ router_weight
        probs = jax.nn.softmax(logits, axis=-1)
        top_p, top_i = jax.lax.top_k(probs, K)
        top_p = top_p / jnp.sum(top_p, axis=-1, keepdims=True)
        exp_idx = top_i.reshape(-1)
        exp_p = top_p.reshape(-1)
        order = jnp.argsort(exp_idx, stable=True)
        sorted_exp = exp_idx[order]
        counts = jnp.bincount(exp_idx, length=E)
        offsets = jnp.concatenate([jnp.zeros((1,), counts.dtype), jnp.cumsum(counts)[:-1]])
        within = jnp.arange(N * K) - offsets[sorted_exp]
        cap = int(np.ceil(N * K / E * CAP_FACTOR))
        T = E * cap
        valid = within < cap
        dst = jnp.where(valid, sorted_exp * cap + within, T)
        padded_tokens = jnp.zeros((T, H), x.dtype).at[dst].set(x[order // K], mode='drop')
        padded_probs = jnp.zeros((T,), exp_p.dtype).at[dst].set(exp_p[order], mode='drop')
        padded_tid = jnp.zeros((T,), jnp.int32).at[dst].set((order // K).astype(jnp.int32), mode='drop')
        xt = padded_tokens.reshape(E, cap, H)
        fc1 = jax.nn.gelu(jnp.einsum('ech,ehf->ecf', xt, moe_w1))
        fc2 = jnp.einsum('ecf,efh->ech', fc1, moe_w2).reshape(T, H)
        weighted = fc2 * padded_probs[:, None]
        moe_out = jnp.zeros((N, H), hidden_states.dtype).at[padded_tid].add(weighted)
        return h1 + moe_out.reshape(S, B, H)

    def _L1_xattn_ref(q, k, v, attn_mask, key_padding_mask, Wq, Wk, Wv, Wo):
        import jax, jax.numpy as jnp
        import numpy as np
        D_MODEL = 128
        N_HEADS = 16
        HEAD_DIM = D_MODEL // N_HEADS
        ROPE_BASE = 10000.0
        NEG_INF = -1000000000.0

        def rotate_half(x):
            x1 = x[..., ::2]
            x2 = x[..., 1::2]
            return jnp.stack((-x2, x1), axis=-1).reshape(x.shape)

        def rope_sin_cos(seq_len, head_dim, dtype):
            inv_freq = 1.0 / ROPE_BASE ** (jnp.arange(0, head_dim, 2, dtype=jnp.float32) / head_dim)
            t = jnp.arange(seq_len, dtype=jnp.float32)
            freqs = jnp.einsum('i,j->ij', t, inv_freq)
            emb = jnp.concatenate((freqs, freqs), axis=-1)
            return (jnp.sin(emb).astype(dtype), jnp.cos(emb).astype(dtype))

        def apply_rope(x, sin, cos):
            return x * cos[None, None] + rotate_half(x) * sin[None, None]
        B, Tq, _ = q.shape
        Tk = k.shape[1]
        H, hd = (N_HEADS, HEAD_DIM)
        qh = (q @ Wq.T).reshape(B, Tq, H, hd).transpose(0, 2, 1, 3)
        kh = (k @ Wk.T).reshape(B, Tk, H, hd).transpose(0, 2, 1, 3)
        vh = (v @ Wv.T).reshape(B, Tk, H, hd).transpose(0, 2, 1, 3)
        sin_q, cos_q = rope_sin_cos(Tq, hd, q.dtype)
        sin_k, cos_k = rope_sin_cos(Tk, hd, k.dtype)
        qh = apply_rope(qh, sin_q, cos_q)
        kh = apply_rope(kh, sin_k, cos_k)
        scores = jnp.einsum('bhqd,bhkd->bhqk', qh, kh) / np.sqrt(hd)
        scores = scores + attn_mask
        scores = jnp.where(key_padding_mask[:, None, None, :], NEG_INF, scores)
        attn = jax.nn.softmax(scores, axis=-1)
        out = jnp.einsum('bhqk,bhkd->bhqd', attn, vh)
        out = out.transpose(0, 2, 1, 3).reshape(B, Tq, H * hd)
        return out @ Wo.T

    def _L1_attn_ref(tokens, norm_w, Wq, Wkv, Wout, q_gamma, k_gamma):
        import jax, jax.numpy as jnp
        import numpy as np
        B, N, D = (2, 256, 128)
        H, QH, DH = (8, 16, 64)
        SOFTCLAMP = 50.0

        def _rmsnorm(x, w):
            eps = jnp.finfo(x.dtype).eps
            return x * jax.lax.rsqrt(jnp.mean(x * x, axis=-1, keepdims=True) + eps) * w

        def _l2norm(x):
            n = jnp.maximum(jnp.linalg.norm(x, axis=-1, keepdims=True), 1e-12)
            return x / n

        def _mh_rmsnorm(x, gamma):
            scale = (gamma + 1.0) * np.sqrt(x.shape[-1]).astype(np.float32)
            return _l2norm(x) * scale[None, :, None, :]
        b, n, d = tokens.shape
        x = _rmsnorm(tokens, norm_w)
        q = (x @ Wq).reshape(b, n, QH, DH).transpose(0, 2, 1, 3)
        kv = x @ Wkv
        k = kv[..., :H * DH].reshape(b, n, H, DH).transpose(0, 2, 1, 3)
        v = kv[..., H * DH:].reshape(b, n, H, DH).transpose(0, 2, 1, 3)
        q = _mh_rmsnorm(q, q_gamma)
        k = _mh_rmsnorm(k, k_gamma)
        g = QH // H
        q = q.reshape(b, H, g, n, DH)
        sim = jnp.einsum('bhgid,bhjd->bhgij', q, k)
        sim = jnp.tanh(sim / SOFTCLAMP) * SOFTCLAMP
        sim = sim * DH ** (-0.5)
        neg = -jnp.finfo(sim.dtype).max
        causal = jnp.triu(jnp.ones((n, n), dtype=bool), 1)
        sim = jnp.where(causal, neg, sim)
        attn = jax.nn.softmax(sim, axis=-1)
        out = jnp.einsum('bhgij,bhjd->bhid', attn, v)
        out = out.transpose(0, 2, 1, 3).reshape(b, n, H * DH)
        return out @ Wout

    def _L1_ffn_ref(x, w1s, w2s, w3s, W1, W2, W3, Wg):
        import jax, jax.numpy as jnp
        import numpy as np
        HIDDEN = 128
        INTER = 512
        N_EXPERTS = 8

        def geglu(x, w1, w2, w3):
            return jax.nn.gelu(x @ w1, approximate=False) * (x @ w2) @ w3
        B, T, C = x.shape
        xf = x.reshape(-1, C)
        shared = geglu(xf, w1s, w2s, w3s)
        logits = xf @ Wg
        idx = jnp.argmax(logits, axis=-1)
        final = jnp.zeros_like(xf)
        for e in range(N_EXPERTS):
            y = geglu(xf, W1[e], W2[e], W3[e])
            final = final + jnp.where((idx == e)[:, None], y, 0.0)
        return (shared + final).reshape(B, T, C)
    x = x + _L0_xattn_ref(_layernorm(x, axis=-1), ctx_1024, ctx_1024, ctx_1024)
    x = x + _L0_attn_ref(_layernorm(x, axis=-1), L0_attn_w_qkv, L0_attn_w_out, L0_attn_b_out)
    x = x + _L0_ffn_ref(_layernorm(x, axis=-1), L0_ffn_ln1_weight, L0_ffn_ln1_bias, L0_ffn_ln2_weight, L0_ffn_ln2_bias, L0_ffn_qkv_weight, L0_ffn_proj_weight, L0_ffn_router_weight, L0_ffn_moe_w1, L0_ffn_moe_w2)
    x = x + _L1_xattn_ref(_layernorm(x, axis=-1), ctx_1024, ctx_1024, mask_1x1xSxS2_fk0, mask_BxS2_bk0, L1_xattn_Wq, L1_xattn_Wk, L1_xattn_Wv, L1_xattn_Wo)
    x = x + _L1_attn_ref(_layernorm(x, axis=-1), L1_attn_norm_w, L1_attn_Wq, L1_attn_Wkv, L1_attn_Wout, L1_attn_q_gamma, L1_attn_k_gamma)
    x = x + _L1_ffn_ref(_layernorm(x, axis=-1), L1_ffn_w1s, L1_ffn_w2s, L1_ffn_w3s, L1_ffn_W1, L1_ffn_W2, L1_ffn_W3, L1_ffn_Wg)
    return x

_drawn_inputs = setup_inputs


def setup_inputs(seed=0):
    import zlib

    import numpy as np

    out = dict(_drawn_inputs(seed))
    spreads = {'L0_ffn_ln1_weight': (1.0, 0.6),
     'L0_ffn_ln1_bias': (0.0, 0.8),
     'L0_ffn_ln2_weight': (1.0, 0.6),
     'L0_ffn_ln2_bias': (0.0, 0.8)}
    factors = {'L0_attn_b_out': 5.889,
     'L0_ffn_qkv_weight': 8.0,
     'L0_ffn_proj_weight': 8.0,
     'L0_ffn_router_weight': 4.916,
     'L0_ffn_moe_w1': 4.277,
     'L0_ffn_moe_w2': 4.181,
     'L1_xattn_Wq': 8.0,
     'L1_xattn_Wk': 8.0,
     'L1_xattn_Wv': 7.037,
     'L1_xattn_Wo': 6.981,
     'L1_attn_norm_w': 8.0,
     'L1_attn_Wq': 3.162,
     'L1_attn_q_gamma': 8.0,
     'L1_attn_k_gamma': 8.0,
     'L1_ffn_w1s': 8.0,
     'L1_ffn_w2s': 8.0,
     'L1_ffn_w3s': 8.0,
     'L1_ffn_W1': 8.0,
     'L1_ffn_W2': 8.0,
     'L1_ffn_W3': 8.0,
     'L1_ffn_Wg': 8.0}
    for name, (base, spread) in spreads.items():
        noise = np.random.default_rng([zlib.crc32(name.encode()), seed]).standard_normal(out[name].shape)
        drawn = base * np.exp(spread * noise) if base else spread * noise
        out[name] = jnp.asarray(drawn.astype(out[name].dtype))
    for name, factor in factors.items():
        out[name] = (out[name] * factor).astype(out[name].dtype)
    return out
```

```python
from contextlib import ExitStack

import numpy as np

import concourse.bass as bass
from concourse import mybir

ALU = mybir.AluOpType
ACT = mybir.ActivationFunctionType
F32 = mybir.dt.float32
U8 = mybir.dt.uint8
U32 = mybir.dt.uint32
AX = mybir.AxisListType.X

P = 128
B, S, D = 128, 32, 128
NT = B * S // P
BT = P // S
J = 257
JC = 86
NJ = 3
JP = NJ * JC
EPS = 1e-5
BIG = 3.0e38
RMS_EPS = float(np.finfo(np.float32).eps)


def steps(eng, n, body, ways=2):
    assert (n - 4) % ways == 0
    for t in range(3):
        body(t, t % ways, t == 0, False)
    with eng.Fori(0, (n - 4) // ways) as i:
        for w in range(ways):
            body(ways * i + 3 + w, (3 + w) % ways, False, False)
    body(n - 1, (n - 1) % ways, False, True)


def wait(eng, sem, value):
    if isinstance(value, int) and value <= 0:
        return
    eng.wait_ge(sem, value)


def wait_apart(eng, sem, value):
    wait(eng, sem, value)
    if not isinstance(value, int):
        eng.wait_ge(sem, 1)


def ts(t, w):
    return bass.ds(t * w, w)


def clear_semaphores(nc, sems):
    with nc.Block() as block:
        @block.sync
        def _(sp):
            for s in sems:
                sp.sem_clear(s)


class Core:

    def __init__(self, nc, ctx):
        self.semaphore = lambda name: ctx.enter_context(nc.semaphore(name))


def residual_tile(dve, k, t, add, chain, done):
    dve.tensor_tensor(k.X[:, t, :], k.X[:, t, :], add, ALU.add).then_inc(chain, 1)
    wait_apart(dve, chain, done + 1)
    dve.bn_stats(k.BNS[:, t, :], k.X[:, t, :]).then_inc(chain, 1)


def deviation_phase(nc, k, name, rms=False):
    with ExitStack() as ctx:
        mv = k.semaphore(f"{name}_mean_var_done")
        sq = k.semaphore(f"{name}_sqrt_done")
        rc = k.semaphore(f"{name}_rstd_done")
        block = ctx.enter_context(nc.Block())

        @block.scalar
        def _(act):
            act.wait_ge(mv, NT)
            act.activation(k.SD[:, :], k.MV[:, :, 1], ACT.Sqrt, bias=k.eps[:, 0:1]).then_inc(sq, 1)
            if rms:
                act.wait_ge(rc, 3)
                act.activation(k.SD[:, :], k.MS[:, :], ACT.Sqrt, bias=k.eps[:, 1:2]).then_inc(sq, 1)

        @block.vector
        def _(dve):
            for t in range(NT):
                dve.bn_aggr(k.MV[:, t, :], k.BNS[:, t, :]).then_inc(mv, 1)
            dve.wait_ge(sq, 1)
            dve.reciprocal(k.RSTD[:, :], k.SD[:, :]).then_inc(rc, 1)
            if rms:
                dve.wait_ge(rc, 1)
                dve.tensor_tensor(k.MS[:, :], k.RSTD[:, :], k.RSTD[:, :], ALU.mult).then_inc(rc, 1)
                dve.wait_ge(rc, 2)
                dve.tensor_tensor(k.MS[:, :], k.MS[:, :], k.MV[:, :, 1], ALU.mult).then_inc(rc, 1)
                dve.wait_ge(sq, 2)
                dve.reciprocal(k.MS[:, :], k.SD[:, :]).then_inc(rc, 1)
                dve.wait_ge(rc, 4)
                dve.tensor_tensor(k.RSTD[:, :], k.RSTD[:, :], k.MS[:, :], ALU.mult).then_inc(rc, 1)


def load_phase(nc, k, x, consts):
    with ExitStack() as ctx:
        xl = k.semaphore("x_loaded")
        cl = k.semaphore("constants_loaded")
        c = k.semaphore("stats0_chain")
        block = ctx.enter_context(nc.Block())

        @block.sync
        def _(sp):
            sp.dma_start(k.X[:, :, :], x.rearrange("(t b) s h -> (b s) t h", b=BT)).then_inc(xl, 16)
            for dst, src in consts:
                sp.dma_start(dst, src).then_inc(cl, 16)
            sp.wait_ge(cl, 16 * len(consts))

        @block.vector
        def _(dve):
            dve.memset(k.eps[:, 0:1], EPS)
            dve.memset(k.eps[:, 1:2], RMS_EPS)
            dve.wait_ge(xl, 16)
            for t in range(NT):
                dve.bn_stats(k.BNS[:, t, :], k.X[:, t, :]).then_inc(c, 1)


def store_phase(nc, k, out):
    with ExitStack() as ctx:
        st = k.semaphore("out_stored")
        block = ctx.enter_context(nc.Block())

        @block.sync
        def _(sp):
            sp.dma_start(out.rearrange("(t b) s h -> (b s) t h", b=BT), k.X[:, :, :]).then_inc(st, 16)
            sp.wait_ge(st, 16)


def stage_ctx_glu(nc, k, ctxT, ctxN):
    with ExitStack() as ctx:
        def sb(name, shape, dt=F32):
            return ctx.enter_context(nc.sbuf_tensor("glu_" + name, shape, dt))

        sems = []

        def sem(name):
            sems.append(ctx.enter_context(nc.semaphore("glu_" + name)))
            return sems[-1]

        WAYS = 4
        cT = [sb(f"ctx_T{i}", [P, BT, JP]) for i in range(WAYS)]
        cN = [sb(f"ctx_N{i}", [JC, BT, NJ, D]) for i in range(WAYS)]
        xn = [sb(f"xn{i}", [P, D]) for i in range(2)]
        xT = [sb(f"xT{i}", [P, P]) for i in range(2)]
        ge = [sb(f"gelu{i}", [JC, BT * NJ * S]) for i in range(2)]
        gh = [sb(f"gh{i}", [JC, BT * NJ * S]) for i in range(2)]
        pT, pH, pY = k.bank[0:2], k.bank[2:4], k.bank[4:6]

        landed = [sem(f"ctx_landed{i}") for i in range(WAYS)]
        normed = sem("x_normed")
        turned = sem("x_transposed")
        xt_ready = sem("xT_copied")
        h_ready = sem("h_ready")
        ge_ready = sem("gelu_ready")
        gh_ready = sem("gh_ready")
        y_ready = sem("y_ready")
        added = sem("residual_chain")
        ctx.callback(clear_semaphores, nc, sems)
        block = ctx.enter_context(nc.Block())

        @block.sync
        def _(sp):
            def load(t, slot):
                sp.dma_start(cT[slot][:, :, :], ctxT[t]).then_inc(landed[slot], 16)
                sp.dma_start(cN[slot][:, :, :, :], ctxN[t]).then_inc(landed[slot], 16)
            for t in range(WAYS):
                load(t, t)
            with sp.Fori(0, NT // WAYS - 1) as i:
                for w in range(WAYS):
                    sp.wait_ge(y_ready, WAYS * i + w + 1)
                    load(WAYS * i + w + WAYS, w)

        @block.tensor
        def _(pe):
            def transpose(t, slot):
                pe.wait_ge(normed, t + 1)
                pe.transpose(pT[slot % 2][:, 0:P], xn[slot % 2][:, :], k.ident[:, :]).then_inc(turned, 1)

            def h(t, slot, half):
                pe.wait_ge(xt_ready, t + 1)
                pe.wait_ge(landed[slot], 32 * (half + 1))
                wait(pe, gh_ready, t - 1)
                for b in range(BT):
                    for c in range(NJ):
                        o = (b * NJ + c) * S
                        m = pe.matmul(pH[slot % 2][0:JC, o:o + S], cT[slot][:, b, c * JC:(c + 1) * JC],
                                      xT[slot % 2][:, b * S:(b + 1) * S], start=True, stop=True)
                m.then_inc(h_ready, 1)

            def y(t, slot):
                pe.wait_ge(gh_ready, t + 1)
                wait(pe, added, 2 * (t - 2) + 1)
                for b in range(BT):
                    for c in range(NJ):
                        o = (b * NJ + c) * S
                        m = pe.matmul(pY[slot % 2][b * S:(b + 1) * S, 0:D], gh[slot % 2][:, o:o + S],
                                      cN[slot][:, b, c, :], start=(c == 0), stop=(c == NJ - 1))
                m.then_inc(y_ready, 1)

            def body(t, slot, first, last):
                if first:
                    transpose(t, slot)
                h(t, slot, t // WAYS if isinstance(t, int) else (t - slot) // WAYS)
                if not last:
                    transpose(t + 1, (slot + 1) % WAYS)
                if not first:
                    y(t - 1, (slot - 1) % WAYS)
                if last:
                    y(t, slot)
            steps(pe, NT, body, WAYS)

        @block.scalar
        def _(act):
            def copy(t, slot):
                act.wait_ge(turned, t + 1)
                wait(act, h_ready, t - 1)
                act.activation(xT[slot % 2][:, :], pT[slot % 2][:, 0:P], ACT.Copy).then_inc(xt_ready, 1)

            def body(t, slot, first, last):
                if first:
                    copy(t, slot)
                act.wait_ge(h_ready, t + 1)
                wait(act, gh_ready, t - 1)
                act.activation(ge[slot % 2][:, :], pH[slot % 2][0:JC, 0:BT * NJ * S], ACT.Gelu).then_inc(ge_ready, 1)
                if not last:
                    copy(t + 1, (slot + 1) % WAYS)
            steps(act, NT, body, WAYS)

        @block.vector
        def _(dve):
            def norm(t, slot):
                wait(dve, turned, t - 1)
                dve.tensor_scalar(xn[slot % 2][:, :], k.X[:, t, :], k.MV[:, t, 0:1], k.RSTD[:, ts(t, 1)],
                                  ALU.subtract, ALU.mult).then_inc(normed, 1)

            def add(t, slot):
                dve.wait_ge(y_ready, t + 1)
                residual_tile(dve, k, t, pY[slot % 2][:, 0:D], added, 2 * t)

            def body(t, slot, first, last):
                if first:
                    norm(t, slot)
                if not last:
                    norm(t + 1, (slot + 1) % WAYS)
                dve.wait_ge(ge_ready, t + 1)
                wait(dve, y_ready, t - 1)
                dve.tensor_tensor(gh[slot % 2][:, :], ge[slot % 2][:, :], pH[slot % 2][0:JC, 0:BT * NJ * S],
                                  ALU.mult).then_inc(gh_ready, 1)
                if not first:
                    add(t - 1, (slot - 1) % WAYS)
                if last:
                    add(t, slot)
            steps(dve, NT, body, WAYS)


def unit(t, h):
    return 2 * t + h


def spread(ap, n):
    return ap.unsqueeze(2).broadcast_to([ap.shape[0], ap.shape[1], n])


def stage_linear_attention(nc, k, wqkv, wout, bout, same_batch):
    H, DH = 16, 64
    HALF = 8
    W = HALF * DH
    NC = W // P
    SCALE = DH ** -0.5
    with ExitStack() as ctx:
        def sb(name, shape, dt=F32):
            return ctx.enter_context(nc.sbuf_tensor("lin_" + name, shape, dt))

        sems = []

        def sem(name):
            sems.append(ctx.enter_context(nc.semaphore("lin_" + name)))
            return sems[-1]

        w = sb("w_qkv", [P, 3, 2, W])
        wo = sb("w_out", [P, 2 * NC, D])
        bo = sb("b_out", [1, D])
        ones = sb("ones", [1, P])
        mask = sb("same_batch", [P, P])
        xn = [sb(f"xn{i}", [P, D]) for i in range(2)]
        xT = [sb(f"xT{i}", [P, P]) for i in range(2)]
        qs = [sb(f"q_exp{i}", [P, HALF, DH]) for i in range(2)]
        qn = [sb(f"q_softmax{i}", [P, HALF, DH]) for i in range(2)]
        qT = [sb(f"q_T{i}", [P, NC, P]) for i in range(2)]
        ks = [sb(f"k_exp{i}", [P, NC, P]) for i in range(2)]
        vs = [sb(f"v{i}", [P, W]) for i in range(2)]
        am = [sb(f"A_T{i}", [P, HALF, P]) for i in range(2)]
        oT = [sb(f"o_T{i}", [P, 2, NC, P]) for i in range(2)]
        qm = [sb(f"q_max{i}", [P, HALF]) for i in range(2)]
        qz = [sb(f"q_sum{i}", [P, HALF]) for i in range(2)]
        rq = [sb(f"q_rsum{i}", [P, HALF]) for i in range(2)]
        km = [sb(f"k_max{i}", [P, NC * BT]) for i in range(2)]
        kz = [sb(f"k_sum{i}", [P, NC * BT]) for i in range(2)]
        rk = [sb(f"k_rsum{i}", [P, NC * BT]) for i in range(2)]
        pQ, pK, pV, pQT, pA0, pA1, pO, pM = k.bank
        pA = (pA0, pA1)
        XC, YC = slice(0, P), slice(P, P + D)

        weights = sem("weights_loaded")
        ones_set = sem("ones_set")
        normed = sem("x_normed")
        turned = sem("x_transposed")
        xt_ready = sem("xT_copied")
        q_made, k_made, v_made = sem("q_made"), sem("k_made"), sem("v_made")
        qmax, qshift, qexp, qsum, qrec, qnorm = (sem(n) for n in (
            "q_max_done", "q_shifted", "q_exp_done", "q_sum_done", "q_recip_done", "q_normed"))
        kmax, kshift, kexp, ksum, krec = (sem(n) for n in (
            "k_max_done", "k_shifted", "k_exp_done", "k_sum_done", "k_recip_done"))
        v_copied = sem("v_copied")
        qt_made, qt_scaled = sem("q_transposed"), sem("qT_scaled")
        a_made, a_masked = sem("A_made"), sem("A_masked")
        o_made, o_copied = sem("o_made"), sem("o_copied")
        y_made = sem("y_made")
        added = sem("residual_chain")
        ctx.callback(clear_semaphores, nc, sems)
        block = ctx.enter_context(nc.Block())

        @block.sync
        def _(sp):
            sp.dma_start(w[:, :, :, :], wqkv).then_inc(weights, 16)
            sp.dma_start(wo[:, :, :], wout).then_inc(weights, 16)
            sp.dma_start(bo[:, :], bout).then_inc(weights, 16)
            sp.dma_start(mask[:, :], same_batch).then_inc(weights, 16)
            sp.wait_ge(weights, 64)

        @block.tensor
        def _(pe):
            def x_transpose(t, slot):
                pe.wait_ge(normed, t + 1)
                wait(pe, added, 2 * (t - 2) + 1)
                pe.transpose(pM[:, XC], xn[slot][:, :], k.ident[:, :]).then_inc(turned, 1)

            def q(t, slot, h):
                u = unit(t, h)
                pe.wait_ge(xt_ready, t + 1)
                wait(pe, qshift, u)
                pe.matmul(pQ[:, :], xT[slot][:, :], w[:, 0, h, :], start=True, stop=True).then_inc(q_made, 1)

            def kk(t, slot, h):
                wait(pe, kshift, unit(t, h))
                for c in range(NC):
                    m = pe.matmul(pK[:, c * P:(c + 1) * P], w[:, 1, h, c * P:(c + 1) * P], xT[slot][:, :],
                                  start=True, stop=True)
                m.then_inc(k_made, 1)

            def v(t, slot, h):
                wait(pe, v_copied, unit(t, h))
                pe.matmul(pV[:, :], xT[slot][:, :], w[:, 2, h, :], start=True, stop=True).then_inc(v_made, 1)

            def q_transpose(t, h):
                u = unit(t, h)
                pe.wait_ge(qnorm, u + 1)
                wait(pe, qt_scaled, u)
                for c in range(NC):
                    m = pe.transpose(pQT[:, c * P:(c + 1) * P], qn[h][:, 2 * c:2 * c + 2, :], k.ident[:, :])
                m.then_inc(qt_made, 1)

            def a(t, h):
                u = unit(t, h)
                pe.wait_ge(qt_scaled, u + 1)
                pe.wait_ge(kexp, u + 1)
                for half in range(2):
                    wait(pe, a_masked, 2 * u - 1 + half)
                    for i in range(4):
                        hd = 2 * i + half
                        r = slice(DH * (hd % 2), DH * (hd % 2) + DH)
                        m = pe.matmul(pA[half][:, i * P:(i + 1) * P], ks[h][r, hd // 2, :], qT[h][r, hd // 2, :],
                                      start=True, stop=True)
                    m.then_inc(a_made, 1)

            def o(t, h):
                u = unit(t, h)
                pe.wait_ge(v_copied, u + 1)
                wait(pe, o_copied, u)
                pe.wait_ge(a_masked, 2 * u + 2)
                for hd in range(HALF):
                    m = pe.matmul(pO[DH * (hd % 2):DH * (hd % 2) + DH, (hd // 2) * P:(hd // 2 + 1) * P],
                                  vs[h][:, hd * DH:(hd + 1) * DH], am[h][:, hd, :], start=True, stop=True)
                m.then_inc(o_made, 1)

            def y(t, slot, last):
                pe.wait_ge(o_copied, 2 * t + 2)
                pe.wait_ge(xt_ready, t + 1 if last else t + 2)
                for c in range(2 * NC):
                    pe.matmul(pM[:, YC], oT[slot][:, c // NC, c % NC, :], wo[:, c, :], start=(c == 0), stop=False)
                pe.matmul(pM[:, YC], ones[:, :], bo[:, :], start=False, stop=True).then_inc(y_made, 1)

            def body(t, slot, first, last):
                if first:
                    pe.wait_ge(weights, 64)
                    pe.wait_ge(ones_set, 1)
                    x_transpose(t, slot)
                for h in range(2):
                    before = (t, 0) if h else (t - 1, 1)
                    if h or not first:
                        q_transpose(*before)
                    q(t, slot, h)
                    kk(t, slot, h)
                    if h or not first:
                        a(*before)
                    v(t, slot, h)
                    if h and not last:
                        x_transpose(t + 1, 1 - slot)
                    if h or not first:
                        o(*before)
                    if not h and not first:
                        y(t - 1, 1 - slot, False)
                if last:
                    q_transpose(t, 1)
                    a(t, 1)
                    o(t, 1)
                    y(t, slot, True)
            steps(pe, NT, body)

        @block.scalar
        def _(act):
            def x_copy(t, slot):
                act.wait_ge(turned, t + 1)
                wait(act, v_made, 2 * (t - 2) + 2)
                act.activation(xT[slot][:, :], pM[:, XC], ACT.Copy).then_inc(xt_ready, 1)

            def o_copy(t, slot, h):
                act.wait_ge(o_made, unit(t, h) + 1)
                wait(act, y_made, t - 1)
                act.activation(oT[slot][:, h, :, :], pO[:, :].rearrange("p (c n) -> p c n", n=P),
                               ACT.Copy).then_inc(o_copied, 1)

            def body(t, slot, first, last):
                if first:
                    x_copy(t, slot)
                for h in range(2):
                    u = unit(t, h)
                    act.wait_ge(qshift, u + 1)
                    act.activation(qs[h][:, :, :], qs[h][:, :, :], ACT.Exp).then_inc(qexp, 1)
                    act.wait_ge(kshift, u + 1)
                    act.activation(ks[h][:, :, :], ks[h][:, :, :], ACT.Exp).then_inc(kexp, 1)
                    act.wait_ge(v_made, u + 1)
                    wait(act, o_made, u - 1)
                    act.activation(vs[h][:, :], pV[:, :], ACT.Copy, scale=SCALE).then_inc(v_copied, 1)
                    if h and not last:
                        x_copy(t + 1, 1 - slot)
                    if h:
                        o_copy(t, slot, 0)
                    elif not first:
                        o_copy(t - 1, 1 - slot, 1)
                if last:
                    o_copy(t, slot, 1)
            steps(act, NT, body)

        @block.gpsimd
        def _(pool):
            pool.memset(ones[:, :], 1.0).then_inc(ones_set, 1)

            def body(t, slot, first, last):
                for h in range(2):
                    u = unit(t, h)
                    pool.wait_ge(qrec, u + 1)
                    wait(pool, qt_made, u - 1)
                    pool.tensor_tensor(qn[h][:, :, :], qs[h][:, :, :], spread(rq[h][:, :], DH),
                                       ALU.mult).then_inc(qnorm, 1)
            steps(pool, NT, body)

        @block.vector
        def _(dve):
            def norm(t, slot):
                wait(dve, turned, t - 1)
                dve.tensor_scalar(xn[slot][:, :], k.X[:, t, :], k.MV[:, t, 0:1], k.RSTD[:, ts(t, 1)],
                                  ALU.subtract, ALU.mult).then_inc(normed, 1)

            def qt_scale(t, h):
                u = unit(t, h)
                dve.wait_ge(qt_made, u + 1)
                wait(dve, a_made, 2 * u - 2)
                dve.wait_ge(krec, u + 1)
                dve.tensor_tensor(qT[h][:, :, :].rearrange("p c (b n) -> p (c b) n", n=S),
                                  pQT[:, :].rearrange("p (c n) -> p c n", n=S), spread(rk[h][:, :], S),
                                  ALU.mult).then_inc(qt_scaled, 1)

            def a_mask(t, h):
                u = unit(t, h)
                wait(dve, o_made, u - 1)
                for half in range(2):
                    dve.wait_ge(a_made, 2 * u + 1 + half)
                    dve.tensor_tensor(am[h][:, half::2, :],
                                      pA[half][:, :].rearrange("p (g n) -> p g n", n=P),
                                      mask[:, :].unsqueeze(1).broadcast_to([P, 4, P]), ALU.mult).then_inc(a_masked, 1)

            def add(t):
                dve.wait_ge(y_made, t + 1)
                residual_tile(dve, k, t, pM[:, YC], added, 2 * t)

            def body(t, slot, first, last):
                if first:
                    dve.wait_ge(weights, 64)
                    norm(t, slot)
                for h in range(2):
                    u = unit(t, h)
                    before = (t, 0) if h else (t - 1, 1)
                    if h == 0 and not last:
                        norm(t + 1, 1 - slot)
                    if h or not first:
                        qt_scale(*before)
                    dve.wait_ge(q_made, u + 1)
                    q3 = pQ[:, :].rearrange("p (g d) -> p g d", d=DH)
                    dve.tensor_reduce(qm[h][:, :], q3, AX, ALU.max).then_inc(qmax, 1)
                    dve.wait_ge(qmax, u + 1)
                    wait(dve, qnorm, u - 1)
                    dve.tensor_tensor(qs[h][:, :, :], q3, spread(qm[h][:, :], DH), ALU.subtract).then_inc(qshift, 1)
                    dve.wait_ge(k_made, u + 1)
                    k3 = pK[:, :].rearrange("p (c n) -> p c n", n=S)
                    dve.tensor_reduce(km[h][:, :], k3, AX, ALU.max).then_inc(kmax, 1)
                    dve.wait_ge(kmax, u + 1)
                    wait(dve, a_made, 2 * u - 2)
                    dve.tensor_tensor(ks[h][:, :, :].rearrange("p c (b n) -> p (c b) n", n=S), k3,
                                      spread(km[h][:, :], S), ALU.subtract).then_inc(kshift, 1)
                    if h or not first:
                        a_mask(*before)
                    dve.wait_ge(qexp, u + 1)
                    dve.tensor_reduce(qz[h][:, :], qs[h][:, :, :], AX, ALU.add).then_inc(qsum, 1)
                    dve.wait_ge(kexp, u + 1)
                    dve.tensor_reduce(kz[h][:, :], ks[h][:, :, :].rearrange("p c (b n) -> p (c b) n", n=S),
                                      AX, ALU.add).then_inc(ksum, 1)
                    dve.wait_ge(qsum, u + 1)
                    dve.reciprocal(rq[h][:, :], qz[h][:, :]).then_inc(qrec, 1)
                    dve.wait_ge(ksum, u + 1)
                    dve.reciprocal(rk[h][:, :], kz[h][:, :]).then_inc(krec, 1)
                    if h == 0 and not first:
                        add(t - 1)
                if last:
                    qt_scale(t, 1)
                    a_mask(t, 1)
                    add(t)
            steps(dve, NT, body)


def stage_clamped_attention(nc, k, wq, wkv, wout, gamma, normw, causal):
    H, DH = 8, 64
    KH = 4
    NQ, NK = H * DH // P, KH * DH // P
    CLAMP = 50.0
    SCALE = DH ** -0.5
    V1 = DH + 1
    with ExitStack() as ctx:
        def sb(name, shape, dt=F32):
            return ctx.enter_context(nc.sbuf_tensor("gqa_" + name, shape, dt))

        sems = []

        def sem(name):
            sems.append(ctx.enter_context(nc.semaphore("gqa_" + name)))
            return sems[-1]

        w_q = sb("w_q", [P, 2, H * DH])
        w_kv = sb("w_kv", [P, 2, 2 * KH * DH])
        wo = sb("w_out", [P, 2 * NK, D])
        gam = sb("gamma", [P, 2 * (NQ + NK)])
        gsc = sb("gamma_scaled", [P, 2 * (NQ + NK)])
        nw = sb("norm_w", [P, 1])
        mask = sb("causal", [P, P])
        half_neg = sb("minus_half", [P, H + KH])
        xn = [sb(f"xn{i}", [P, D]) for i in range(2)]
        xT = [sb(f"xT{i}", [P, P]) for i in range(2)]
        sq = [sb(f"squares{i}", [P, (H + KH) * DH]) for i in range(2)]
        ss = [sb(f"norm2{i}", [P, H + KH]) for i in range(2)]
        sm = [sb(f"norm2_min{i}", [P, H + KH]) for i in range(2)]
        rn = [sb(f"rnorm{i}", [P, H + KH]) for i in range(2)]
        qk = [sb(f"qk_unit{i}", [P, (H + KH) * DH]) for i in range(2)]
        qkT = [sb(f"qk_T{i}", [P, NQ + NK, P]) for i in range(2)]
        va = [sb(f"v_ones{i}", [P, KH, V1]) for i in range(2)]
        th = [sb(f"tanh{i}", [P, 4 * P]) for i in range(2)]
        ex = [sb(f"exp{i}", [P, 4, P]) for i in range(2)]
        pm = [sb(f"p{i}", [P, H, P]) for i in range(2)]
        rs = [sb(f"p_rsum{i}", [P, 4]) for i in range(2)]
        on = [sb(f"o_head{i}", [P, 4, DH]) for i in range(2)]
        os_ = [sb(f"o{i}", [P, 2, KH, DH]) for i in range(2)]
        oT = [sb(f"o_T{i}", [P, 4 * P]) for i in range(2)]
        pQ, pKV, pT0, pT1, pS0, pS1, pO, pM = k.bank
        pS = (pS0, pS1)
        XC, YC = slice(0, P), slice(P, P + D)

        weights = sem("weights_loaded")
        const_set = sem("constants_set")
        gamma_done = sem("gamma_done")
        normed, turned, xt_ready = sem("x_normed"), sem("x_transposed"), sem("xT_copied")
        q_made, kv_made = sem("q_made"), sem("kv_made")
        copied, squared, v_copied = sem("qk_copied"), sem("squared"), sem("v_copied")
        ssum, smin, rnorm, scaled = sem("norm2_done"), sem("norm2_min_done"), sem("rnorm_done"), sem("qk_scaled")
        t_made, t_copied = sem("qk_transposed"), sem("qkT_copied")
        s_made, tanhed, exped, masked = sem("scores_made"), sem("tanh_done"), sem("exp_done"), sem("p_masked")
        pv_made, recip, onorm, osum = sem("pv_made"), sem("recip_done"), sem("o_normed"), sem("o_summed")
        ot_made, ot_copied, y_made = sem("o_transposed"), sem("oT_copied"), sem("y_made")
        added = sem("residual_chain")
        ctx.callback(clear_semaphores, nc, sems)
        block = ctx.enter_context(nc.Block())

        @block.sync
        def _(sp):
            for dst, src in ((w_q[:, :, :], wq), (w_kv[:, :, :], wkv), (wo[:, :, :], wout), (gam[:, :], gamma),
                             (nw[:, :], normw), (mask[:, :], causal)):
                sp.dma_start(dst, src).then_inc(weights, 16)
            sp.wait_ge(weights, 96)

        @block.tensor
        def _(pe):
            def x_transpose(t, slot):
                pe.wait_ge(normed, t + 1)
                wait(pe, added, 2 * (t - 3) + 1)
                pe.transpose(pM[:, XC], xn[slot][:, :], k.ident[:, :]).then_inc(turned, 1)

            def qk_transpose(t, h):
                u = unit(t, h)
                pe.wait_ge(scaled, 2 * u + 2)
                wait(pe, t_copied, 2 * u)
                wait(pe, ot_copied, t - 1 + h)
                for c in range(NQ + NK):
                    dst = pT0 if c < NQ else pT1
                    o = (c % NQ) * P
                    m = pe.transpose(dst[:, o:o + P], qk[h][:, c * P:(c + 1) * P], k.ident[:, :])
                m.then_inc(t_made, 1)

            def q(t, slot, h):
                pe.wait_ge(xt_ready, t + 1)
                wait(pe, squared, 2 * unit(t, h) - 1)
                pe.matmul(pQ[:, :], xT[slot][:, :], w_q[:, h, :], start=True, stop=True).then_inc(q_made, 1)

            def kv(t, slot, h):
                u = unit(t, h)
                wait(pe, v_copied, u)
                pe.matmul(pKV[:, :], xT[slot][:, :], w_kv[:, h, :], start=True, stop=True).then_inc(kv_made, 1)

            def scores(t, h):
                u = unit(t, h)
                pe.wait_ge(t_copied, 2 * u + 2)
                for part in range(2):
                    wait(pe, tanhed, 2 * u - 1 + part)
                    for i in range(4):
                        kh, g = part + 2 * (i // 2), i % 2
                        r = slice(DH * (kh % 2), DH * (kh % 2) + DH)
                        m = pe.matmul(pS[part][:, i * P:(i + 1) * P], qkT[h][r, NQ + kh // 2, :],
                                      qkT[h][r, 2 * (kh // 2) + g, :], start=True, stop=True)
                    m.then_inc(s_made, 1)

            def pv(t, h, part):
                n = 2 * unit(t, h) + part
                pe.wait_ge(masked, n + 1)
                wait(pe, onorm, n)
                for i in range(4):
                    hd = 4 * part + i
                    m = pe.matmul(pO[:, i * V1:(i + 1) * V1], pm[h][:, hd, :], va[h][:, part + 2 * (i // 2), :],
                                  start=True, stop=True)
                m.then_inc(pv_made, 1)

            def o_transpose(t, slot, last):
                pe.wait_ge(osum, 4 * t + 4)
                pe.wait_ge(t_copied, 4 * t + 4 if last else 4 * t + 5)
                for c in range(2 * NK):
                    m = pe.transpose(pT0[:, c * P:(c + 1) * P], os_[slot][:, c // NK, 2 * (c % NK):2 * (c % NK) + 2, :],
                                     k.ident[:, :])
                m.then_inc(ot_made, 1)

            def y(t, slot, last):
                pe.wait_ge(ot_copied, t + 1)
                pe.wait_ge(xt_ready, NT if last else t + 3)
                for c in range(2 * NK):
                    m = pe.matmul(pM[:, YC], oT[slot][:, c * P:(c + 1) * P], wo[:, c, :],
                                  start=(c == 0), stop=(c == 2 * NK - 1))
                m.then_inc(y_made, 1)

            def body(t, slot, first, last):
                if first:
                    pe.wait_ge(weights, 96)
                    pe.wait_ge(const_set, 3)
                    x_transpose(t, slot)
                third = not isinstance(t, int) or t >= 2
                for h in range(2):
                    q(t, slot, h)
                    kv(t, slot, h)
                    if not first:
                        pv(t - 1, h, 0)
                    if h or not first:
                        qk_transpose(*((t, 0) if h else (t - 1, 1)))
                    if not first:
                        pv(t - 1, h, 1)
                    if not h and third:
                        y(t - 2, slot, False)
                    if h and not last:
                        x_transpose(t + 1, 1 - slot)
                    if h or not first:
                        scores(*((t, 0) if h else (t - 1, 1)))
                    if h and not first:
                        o_transpose(t - 1, 1 - slot, False)
                if last:
                    y(t - 1, 1 - slot, True)
                    qk_transpose(t, 1)
                    pv(t, 0, 0)
                    pv(t, 0, 1)
                    scores(t, 1)
                    pv(t, 1, 0)
                    pv(t, 1, 1)
                    o_transpose(t, slot, True)
                    y(t, slot, True)
            steps(pe, NT, body)

        @block.scalar
        def _(act):
            def x_copy(t, slot):
                act.wait_ge(turned, t + 1)
                wait(act, kv_made, 2 * (t - 2) + 2)
                act.activation(xT[slot][:, :], pM[:, XC], ACT.Copy, scale=nw[:, 0:1]).then_inc(xt_ready, 1)

            def probs(t, h):
                for part in range(2):
                    n = 2 * unit(t, h) + part
                    act.wait_ge(s_made, n + 1)
                    act.activation(th[part][:, :], pS[part][:, :], ACT.Tanh, scale=1.0 / CLAMP).then_inc(tanhed, 1)
                    act.wait_ge(tanhed, n + 1)
                    wait(act, masked, n - 1)
                    act.activation(ex[part][:, :, :], th[part][:, :].rearrange("p (g n) -> p g n", n=P), ACT.Exp,
                                   scale=CLAMP * SCALE).then_inc(exped, 1)

            def o_copy(t, slot):
                act.wait_ge(ot_made, t + 1)
                wait(act, y_made, t - 1)
                act.activation(oT[slot][:, :], pT0[:, :], ACT.Copy).then_inc(ot_copied, 1)

            def body(t, slot, first, last):
                if first:
                    act.wait_ge(weights, 96)
                    x_copy(t, slot)
                for h in range(2):
                    u = unit(t, h)
                    act.wait_ge(q_made, u + 1)
                    wait(act, t_made, u - 1)
                    act.activation(qk[h][:, 0:H * DH], pQ[:, :], ACT.Copy).then_inc(copied, 1)
                    wait(act, ssum, u - 1)
                    act.activation(sq[h][:, 0:H * DH], pQ[:, :], ACT.Square).then_inc(squared, 1)
                    act.wait_ge(kv_made, u + 1)
                    act.activation(qk[h][:, H * DH:], pKV[:, 0:KH * DH], ACT.Copy).then_inc(copied, 1)
                    act.activation(sq[h][:, H * DH:], pKV[:, 0:KH * DH], ACT.Square).then_inc(squared, 1)
                    if first:
                        act.wait_ge(const_set, 3)
                    wait(act, pv_made, 2 * u - 2)
                    act.activation(va[h][:, :, 0:DH], pKV[:, KH * DH:].rearrange("p (g d) -> p g d", d=DH),
                                   ACT.Copy).then_inc(v_copied, 1)
                    if h or not first:
                        probs(*((t, 0) if h else (t - 1, 1)))
                    if h and not last:
                        x_copy(t + 1, 1 - slot)
                    if h and not first:
                        o_copy(t - 1, 1 - slot)
                if last:
                    probs(t, 1)
                    o_copy(t, slot)
            steps(act, NT, body)

        @block.gpsimd
        def _(pool):
            def o_sum(t, slot, h, part):
                n = 2 * unit(t, h) + part
                pool.wait_ge(onorm, n + 1)
                if h == 0 and part == 0:
                    wait(pool, ot_made, t - 1)
                o4 = on[part][:, :, :].rearrange("p (k g) d -> p k g d", g=2)
                pool.tensor_tensor(os_[slot][:, h, part::2, :], o4[:, :, 0, :], o4[:, :, 1, :],
                                   ALU.add).then_inc(osum, 1)

            def p_mask(t, h):
                for part in range(2):
                    n = 2 * unit(t, h) + part
                    pool.wait_ge(exped, n + 1)
                    wait(pool, pv_made, n - 3)
                    pool.tensor_tensor(pm[h][:, 4 * part:4 * part + 4, :], ex[part][:, :, :],
                                       mask[:, :].unsqueeze(1).broadcast_to([P, 4, P]), ALU.mult).then_inc(masked, 1)

            def body(t, slot, first, last):
                if first:
                    pool.wait_ge(weights, 96)
                    for i in range(2):
                        pool.memset(va[i][:, :, DH:V1], 1.0).then_inc(const_set, 1)
                    pool.memset(half_neg[:, :], -0.5).then_inc(const_set, 1)
                    pool.wait_ge(const_set, 3)
                for h in range(2):
                    u = unit(t, h)
                    pool.wait_ge(smin, u + 1)
                    wait(pool, scaled, 2 * u - 2)
                    pool.tensor_tensor(rn[h][:, :], sm[h][:, :], half_neg[:, :], ALU.pow).then_inc(rnorm, 1)
                    if not first:
                        o_sum(t - 1, 1 - slot, h, 0)
                        o_sum(t - 1, 1 - slot, h, 1)
                    if h or not first:
                        p_mask(*((t, 0) if h else (t - 1, 1)))
                if last:
                    o_sum(t, slot, 0, 0)
                    o_sum(t, slot, 0, 1)
                    p_mask(t, 1)
                    o_sum(t, slot, 1, 0)
                    o_sum(t, slot, 1, 1)
            steps(pool, NT, body)

        @block.vector
        def _(dve):
            def norm(t, slot):
                wait(dve, turned, t - 1)
                dve.tensor_scalar(xn[slot][:, :], k.X[:, t, :], k.MV[:, t, 0:1], k.RSTD[:, ts(t, 1)],
                                  ALU.subtract, ALU.mult).then_inc(normed, 1)

            def t_copy(t, h):
                u = unit(t, h)
                dve.wait_ge(t_made, u + 1)
                wait(dve, s_made, 2 * u - 2)
                g0 = (NQ + NK) * h
                for lo, n, src in ((0, NQ, pT0), (NQ, NK, pT1)):
                    dve.tensor_tensor(qkT[h][:, lo:lo + n, :], src[:, 0:n * P].rearrange("p (c n) -> p c n", n=P),
                                      spread(gsc[:, g0 + lo:g0 + lo + n], P), ALU.mult).then_inc(t_copied, 1)

            def o_norm(t, h, part):
                n = 2 * unit(t, h) + part
                dve.wait_ge(pv_made, n + 1)
                o3 = pO[:, 0:4 * V1].rearrange("p (g d) -> p g d", d=V1)
                dve.reciprocal(rs[part][:, :], o3[:, :, DH]).then_inc(recip, 1)
                dve.wait_ge(recip, n + 1)
                wait(dve, osum, n - 1)
                dve.tensor_tensor(on[part][:, :, :], o3[:, :, 0:DH], spread(rs[part][:, :], DH),
                                  ALU.mult).then_inc(onorm, 1)

            def add(t):
                dve.wait_ge(y_made, t + 1)
                residual_tile(dve, k, t, pM[:, YC], added, 2 * t)

            def body(t, slot, first, last):
                if first:
                    dve.wait_ge(weights, 96)
                    dve.tensor_scalar(gsc[:, :], gam[:, :], 1.0, float(DH) ** 0.5, ALU.add,
                                      ALU.mult).then_inc(gamma_done, 1)
                    dve.wait_ge(gamma_done, 1)
                    norm(t, slot)
                for h in range(2):
                    u = unit(t, h)
                    if h == 0 and not last:
                        norm(t + 1, 1 - slot)
                    dve.wait_ge(squared, 2 * u + 2)
                    dve.tensor_reduce(ss[h][:, :], sq[h][:, :].rearrange("p (g d) -> p g d", d=DH), AX,
                                      ALU.add).then_inc(ssum, 1)
                    dve.wait_ge(ssum, u + 1)
                    wait(dve, rnorm, u - 1)
                    dve.tensor_scalar(sm[h][:, :], ss[h][:, :], 1e-24, None, ALU.max).then_inc(smin, 1)
                    if not first:
                        o_norm(t - 1, h, 0)
                    if h or not first:
                        t_copy(*((t, 0) if h else (t - 1, 1)))
                    if not first:
                        o_norm(t - 1, h, 1)
                    dve.wait_ge(rnorm, u + 1)
                    dve.wait_ge(copied, 2 * u + 2)
                    q3 = qk[h][:, 0:H * DH].rearrange("p (g d) -> p g d", d=DH)
                    k3 = qk[h][:, H * DH:].rearrange("p (g d) -> p g d", d=DH)
                    dve.tensor_tensor(q3, q3, spread(rn[h][:, 0:H], DH), ALU.mult).then_inc(scaled, 1)
                    dve.tensor_tensor(k3, k3, spread(rn[h][:, H:H + KH], DH), ALU.mult).then_inc(scaled, 1)
                    if not h and (not isinstance(t, int) or t >= 2):
                        add(t - 2)
                if last:
                    add(t - 1)
                    t_copy(t, 1)
                    o_norm(t, 0, 0)
                    o_norm(t, 0, 1)
                    o_norm(t, 1, 0)
                    o_norm(t, 1, 1)
                    add(t)
            steps(dve, NT, body)


def stage_hidden(nc, k):
    with ExitStack() as ctx:
        normed = k.semaphore("hid_normed")
        stats = k.semaphore("hid_stats_done")
        block = ctx.enter_context(nc.Block())

        @block.vector
        def _(dve):
            def norm(t):
                dve.tensor_scalar(k.HID[:, t, :], k.X[:, t, :], k.MV[:, t, 0:1], k.RSTD[:, ts(t, 1)],
                                  ALU.subtract, ALU.mult).then_inc(normed, 1)

            def body(t, slot, first, last):
                if first:
                    norm(t)
                if not last:
                    norm(t + 1)
                wait_apart(dve, normed, t + 1)
                dve.bn_stats(k.BNS[:, t, :], k.HID[:, t, :]).then_inc(stats, 1)
            steps(dve, NT, body)


def stage_norm_transpose(nc, k, name, src, affine, router=None):
    with ExitStack() as ctx:
        def sb(nm, shape, dt=F32):
            return ctx.enter_context(nc.sbuf_tensor(f"{name}_{nm}", shape, dt))

        def sem(nm):
            return k.semaphore(f"{name}_{nm}")

        xn = [sb(f"xn{i}", [P, D]) for i in range(2)]
        xT = [sb(f"xT{i}", [P, P]) for i in range(2)]
        wr = sb("router", [P, 8])
        wb = sb("weight_bias", [P, 2])
        pT, pL = k.bank[0:2], k.bank[2:4]
        loads = [(wb[:, :], affine)] if affine is not None else []
        loads += [(wr[:, :], router)] if router is not None else []
        weights = sem("weights_loaded")
        normed, turned, copied, kept = sem("normed"), sem("transposed"), sem("copied"), sem("kept")
        l_made, l_copied = sem("logits_made"), sem("logits_copied")
        block = ctx.enter_context(nc.Block())

        if loads:
            @block.sync
            def _(sp):
                for dst, s in loads:
                    sp.dma_start(dst, s).then_inc(weights, 16)
                sp.wait_ge(weights, 16 * len(loads))

        @block.tensor
        def _(pe):
            def logits(t, slot):
                pe.wait_ge(copied, t + 1)
                wait(pe, l_copied, t - 1)
                pe.matmul(pL[slot][:, 0:8], xT[slot][:, :], wr[:, :], start=True, stop=True).then_inc(l_made, 1)

            def body(t, slot, first, last):
                if first and loads:
                    pe.wait_ge(weights, 16 * len(loads))
                pe.wait_ge(normed, t + 1)
                wait(pe, copied, t - 1)
                pe.transpose(pT[slot][:, 0:P], xn[slot][:, :], k.ident[:, :]).then_inc(turned, 1)
                if router is not None:
                    if not first:
                        logits(t - 1, 1 - slot)
                    if last:
                        logits(t, slot)
            steps(pe, NT, body)

        @block.scalar
        def _(act):
            def body(t, slot, first, last):
                if first and loads:
                    act.wait_ge(weights, 16 * len(loads))
                act.wait_ge(turned, t + 1)
                wait(act, kept, t - 1)
                if router is not None:
                    wait(act, l_made, t - 1)
                if affine is not None:
                    act.activation(xT[slot][:, :], pT[slot][:, 0:P], ACT.Identity, bias=wb[:, 1:2],
                                   scale=wb[:, 0:1]).then_inc(copied, 1)
                else:
                    act.activation(xT[slot][:, :], pT[slot][:, 0:P], ACT.Copy).then_inc(copied, 1)
            steps(act, NT, body)

        @block.gpsimd
        def _(pool):
            def body(t, slot, first, last):
                wait_apart(pool, copied, t + 1)
                pool.tensor_copy(k.LT[:, t, :], xT[slot][:, :]).then_inc(kept, 1)
            steps(pool, NT, body)

        @block.vector
        def _(dve):
            def norm(t, slot):
                wait(dve, turned, t - 1)
                dve.tensor_scalar(xn[slot][:, :], src[:, t, :], k.MV[:, t, 0:1], k.RSTD[:, ts(t, 1)],
                                  ALU.subtract, ALU.mult).then_inc(normed, 1)

            def body(t, slot, first, last):
                if first:
                    norm(t, slot)
                if not last:
                    norm(t + 1, 1 - slot)
                if router is not None:
                    dve.wait_ge(l_made, t + 1)
                    if not isinstance(t, int):
                        dve.wait_ge(l_made, 1)
                    dve.tensor_copy(k.LG[:, t, :], pL[slot][:, 0:8]).then_inc(l_copied, 1)
            steps(dve, NT, body)


def stage_batch_attention(nc, k, wq, wkr, wv, head_diag, causal_add):
    G, QH, HD = 4, 4, 8
    V1 = HD + 1
    SCALE = HD ** -0.5
    with ExitStack() as ctx:
        def sb(name, shape, dt=F32):
            return ctx.enter_context(nc.sbuf_tensor("bat_" + name, shape, dt))

        sems = []

        def sem(name):
            sems.append(ctx.enter_context(nc.semaphore("bat_" + name)))
            return sems[-1]

        w_q, w_k, w_v = sb("w_q", [P, P]), sb("w_k", [P, P]), sb("w_v", [P, G * HD])
        hdiag = sb("head_diag", [P, QH])
        cadd = sb("causal_add", [P, P])
        ls = [sb(f"ln_s{i}", [P, P]) for i in range(2)]
        qT = [sb(f"q_T{i}", [P, P]) for i in range(2)]
        kb = [sb(f"k_blocks{i}", [P, QH, P]) for i in range(2)]
        va = [sb(f"v_ones{i}", [P, G, V1]) for i in range(2)]
        sx = [sb(f"scores{g}", [P, QH, P]) for g in range(G)]
        mx = [sb(f"max{g}", [P, QH]) for g in range(G)]
        pt = [sb(f"p_T{g}", [P, QH * P]) for g in range(G)]
        rs = sb("rsum", [P, G * QH])
        ao = sb("o", [P, G * QH, HD])
        pF, pK, pS0, pS1, pT0, pT1, pO, pM = k.bank
        pS, pT = (pS0, pS1), (pT0, pT1)
        ALLT = k.LT[:, :, :].rearrange("p t (b s) -> p (t b) s", s=S)
        ALLA = k.AT[:, :, :].rearrange("p t (b s) -> p (t b) s", s=S)

        weights, ones_set = sem("weights_loaded"), sem("ones_set")
        staged = sem("ln_staged")
        k_made, v_made = sem("k_made"), sem("v_made")
        q_copied, v_copied, k_spread = sem("q_copied"), sem("v_copied"), sem("k_spread")
        s_made, s_added, s_max, s_shifted, s_exp = (sem(n) for n in (
            "scores_made", "scores_masked", "max_done", "scores_shifted", "exp_done"))
        t_made, t_copied, pv_made = sem("p_transposed"), sem("pT_copied"), sem("pv_made")
        recip, o_normed, ot_made, ot_copied = sem("recip_done"), sem("o_normed"), sem("o_transposed"), sem("oT_copied")
        ctx.callback(clear_semaphores, nc, sems)
        block = ctx.enter_context(nc.Block())

        def ago(s, g, n):
            d = g - n
            return (s + d // G, d % G, G * s + d)

        @block.sync
        def _(sp):
            for dst, src in ((w_q[:, :], wq), (w_k[:, :], wkr), (w_v[:, :], wv), (hdiag[:, :], head_diag),
                             (cadd[:, :], causal_add)):
                sp.dma_start(dst, src).then_inc(weights, 16)
            sp.wait_ge(weights, 80)

        @block.tensor
        def _(pe):
            def front(s, slot):
                pe.wait_ge(staged, s + 1)
                wait(pe, v_copied, s)
                pe.matmul(pF[:, 0:P], w_q[:, :], ls[slot][:, :], start=True, stop=True)
                pe.matmul(pF[:, P:P + G * HD], ls[slot][:, :], w_v[:, :], start=True, stop=True).then_inc(v_made, 1)
                wait(pe, k_spread, s)
                pe.matmul(pK[:, 0:P], w_k[:, :], ls[slot][:, :], start=True, stop=True).then_inc(k_made, 1)

            def scores(s, slot, g):
                n = G * s + g
                pe.wait_ge(q_copied, s + 1)
                pe.wait_ge(k_spread, s + 1)
                wait(pe, s_added, n - 1)
                r = slice(32 * g, 32 * g + 32)
                pe.matmul(pS[g % 2][:, :], qT[slot][r, :], kb[slot][r, :, :], start=True, stop=True)\
                    .then_inc(s_made, 1)

            def p_transpose(g, n):
                pe.wait_ge(s_exp, n + 1)
                wait(pe, t_copied, n - 1)
                for i in range(QH):
                    m = pe.transpose(pT[g % 2][:, i * P:(i + 1) * P], sx[g][:, i, :], k.ident[:, :])
                m.then_inc(t_made, 1)

            def pv(s, g, n, slot):
                pe.wait_ge(t_copied, n + 1)
                pe.wait_ge(v_copied, s + 1)
                if g == 0:
                    wait(pe, o_normed, s)
                for i in range(QH):
                    o = (g * QH + i) * V1
                    m = pe.matmul(pO[:, o:o + V1], pt[g][:, i * P:(i + 1) * P], va[slot][:, g, :],
                                  start=True, stop=True)
                m.then_inc(pv_made, 1)

            def o_transpose(s):
                pe.wait_ge(o_normed, s + 1)
                wait(pe, ot_copied, s)
                pe.transpose(pM[:, 0:P], ao[:, :, :], k.ident[:, :]).then_inc(ot_made, 1)

            def body(s, slot, first, last):
                if first:
                    pe.wait_ge(weights, 80)
                    pe.wait_ge(ones_set, 2)
                    front(s, slot)
                for g in range(G):
                    scores(s, slot, g)
                    if not (first and g < 2):
                        _, g2, n2 = ago(s, g, 2)
                        p_transpose(g2, n2)
                    if not (first and g < 3):
                        s3, g3, n3 = ago(s, g, 3)
                        pv(s3, g3, n3, slot if g == 3 else 1 - slot)
                    if g == 2 and not last:
                        front(s + 1, 1 - slot)
                    if g == 3 and not first:
                        o_transpose(s - 1)
                if last:
                    for g in range(2, 4):
                        p_transpose(g, G * s + g)
                    for g in range(1, 4):
                        pv(s, g, G * s + g, slot)
                    o_transpose(s)
            steps(pe, S, body)

        @block.scalar
        def _(act):
            def front(s, slot):
                act.wait_ge(v_made, s + 1)
                wait(act, s_made, G * (s - 1))
                act.activation(qT[slot][:, :], pF[:, 0:P], ACT.Copy, scale=SCALE).then_inc(q_copied, 1)
                wait(act, pv_made, G * (s - 1))
                act.activation(va[slot][:, :, 0:HD], pF[:, P:P + G * HD].rearrange("p (g d) -> p g d", d=HD),
                               ACT.Copy).then_inc(v_copied, 1)

            def exp(g, n):
                act.wait_ge(s_shifted, n + 1)
                act.activation(sx[g][:, :, :], sx[g][:, :, :], ACT.Exp).then_inc(s_exp, 1)

            def t_copy(g, n):
                act.wait_ge(t_made, n + 1)
                wait(act, pv_made, n - 3)
                act.activation(pt[g][:, :], pT[g % 2][:, :], ACT.Copy).then_inc(t_copied, 1)

            def o_copy(s):
                wait_apart(act, ot_made, s + 1)
                act.activation(ALLA[:, :, s], pM[:, 0:P], ACT.Copy).then_inc(ot_copied, 1)

            def body(s, slot, first, last):
                if first:
                    act.wait_ge(ones_set, 2)
                    front(s, slot)
                for g in range(G):
                    if not (first and g < 1):
                        _, g1, n1 = ago(s, g, 1)
                        exp(g1, n1)
                    if not (first and g < 2):
                        _, g2, n2 = ago(s, g, 2)
                        t_copy(g2, n2)
                    if g == 3 and not last:
                        front(s + 1, 1 - slot)
                    if g == 3 and not first:
                        o_copy(s - 1)
                if last:
                    exp(3, G * s + 3)
                    t_copy(2, G * s + 2)
                    t_copy(3, G * s + 3)
                    o_copy(s)
            steps(act, S, body)

        @block.gpsimd
        def _(pool):
            def stage(s, slot):
                wait_apart(pool, k_made, s - 1)
                pool.tensor_copy(ls[slot][:, :], ALLT[:, :, s]).then_inc(staged, 1)

            def body(s, slot, first, last):
                if first:
                    for i in range(2):
                        pool.memset(va[i][:, :, HD:V1], 1.0).then_inc(ones_set, 1)
                    stage(s, slot)
                for g in range(G):
                    n = G * s + g
                    pool.wait_ge(s_max, n + 1)
                    pool.tensor_tensor(sx[g][:, :, :], sx[g][:, :, :], spread(mx[g][:, :], P),
                                       ALU.subtract).then_inc(s_shifted, 1)
                    if g == 0 and not last:
                        stage(s + 1, 1 - slot)
            steps(pool, S, body)

        @block.vector
        def _(dve):
            def spread_k(s, slot):
                dve.wait_ge(k_made, s + 1)
                wait(dve, s_made, G * (s - 1))
                dve.tensor_tensor(kb[slot][:, :, :], pK[:, 0:P].unsqueeze(1).broadcast_to([P, QH, P]),
                                  spread(hdiag[:, :], P), ALU.mult).then_inc(k_spread, 1)

            def o_norm(s):
                dve.wait_ge(pv_made, G * s + G)
                o3 = pO[:, 0:G * QH * V1].rearrange("p (g d) -> p g d", d=V1)
                dve.reciprocal(rs[:, :], o3[:, :, HD]).then_inc(recip, 1)
                dve.wait_ge(recip, s + 1)
                wait(dve, ot_made, s)
                dve.tensor_tensor(ao[:, :, :], o3[:, :, 0:HD], spread(rs[:, :], HD), ALU.mult).then_inc(o_normed, 1)

            def body(s, slot, first, last):
                if first:
                    dve.wait_ge(weights, 80)
                    spread_k(s, slot)
                for g in range(G):
                    n = G * s + g
                    dve.wait_ge(s_made, n + 1)
                    wait(dve, t_made, n - 3)
                    dve.tensor_tensor(sx[g][:, :, :], pS[g % 2][:, :].rearrange("p (i n) -> p i n", n=P),
                                      cadd[:, :].unsqueeze(1).broadcast_to([P, QH, P]), ALU.add).then_inc(s_added, 1)
                    dve.wait_ge(s_added, n + 1)
                    dve.tensor_reduce(mx[g][:, :], sx[g][:, :, :], AX, ALU.max).then_inc(s_max, 1)
                    if g == 2 and not first:
                        o_norm(s - 1)
                    if g == 3 and not last:
                        spread_k(s + 1, 1 - slot)
                if last:
                    o_norm(s)
            steps(dve, S, body)


def stage_projection(nc, k, wproj):
    with ExitStack() as ctx:
        def sb(name, shape, dt=F32):
            return ctx.enter_context(nc.sbuf_tensor("prj_" + name, shape, dt))

        def sem(name):
            return k.semaphore("prj_" + name)

        w = sb("w", [P, D])
        at = [sb(f"o_T{i}", [P, P]) for i in range(2)]
        pY = k.bank[0:2]
        weights, staged, made, chain, summed = (sem(n) for n in (
            "weights_loaded", "o_staged", "made", "chain", "x_summed"))
        block = ctx.enter_context(nc.Block())

        @block.sync
        def _(sp):
            sp.dma_start(w[:, :], wproj).then_inc(weights, 16)
            sp.wait_ge(weights, 16)

        @block.scalar
        def _(act):
            def body(t, slot, first, last):
                wait_apart(act, made, t - 1)
                act.activation(at[slot][:, :], k.AT[:, t, :], ACT.Copy).then_inc(staged, 1)
            steps(act, NT, body)

        @block.tensor
        def _(pe):
            def body(t, slot, first, last):
                if first:
                    pe.wait_ge(weights, 16)
                pe.wait_ge(staged, t + 1)
                wait(pe, chain, 2 * (t - 2) + 1)
                pe.matmul(pY[slot][:, 0:D], at[slot][:, :], w[:, :], start=True, stop=True).then_inc(made, 1)
            steps(pe, NT, body)

        @block.vector
        def _(dve):
            def body(t, slot, first, last):
                dve.wait_ge(made, t + 1)
                dve.tensor_tensor(k.HID[:, t, :], k.HID[:, t, :], pY[slot][:, 0:D], ALU.add).then_inc(chain, 1)
                wait_apart(dve, chain, 2 * t + 1)
                dve.bn_stats(k.BNS[:, t, :], k.HID[:, t, :]).then_inc(chain, 1)
            steps(dve, NT, body)

        @block.gpsimd
        def _(pool):
            def body(t, slot, first, last):
                wait_apart(pool, chain, 2 * t + 1)
                pool.tensor_tensor(k.X[:, t, :], k.X[:, t, :], k.HID[:, t, :], ALU.add).then_inc(summed, 1)
            steps(pool, NT, body)


def first_of(dve, link, tmp, onehot, values, top, down):
    link(dve.tensor_tensor(tmp, values, spread(top, 8), ALU.is_equal))
    link(dve.tensor_tensor(tmp, tmp, down.unsqueeze(1).broadcast_to([P, NT, 8]), ALU.mult))
    link(dve.tensor_reduce(top, tmp, AX, ALU.max))
    link(dve.tensor_tensor(onehot, tmp, spread(top, 8), ALU.is_equal))


def stage_route_two(nc, k, earlier, countdown):
    E = 8
    CAP = -(-(B * S * 2 * 5) // (E * 4))
    with ExitStack() as ctx:
        def sb(name, shape, dt=F32):
            return ctx.enter_context(nc.sbuf_tensor("top2_" + name, shape, dt))

        def sem(name):
            return k.semaphore("top2_" + name)

        low = sb("earlier_rows", [P, P])
        ones = sb("ones", [P, P])
        down = sb("countdown", [P, E])
        top, top2, tot = sb("top", [P, NT]), sb("top2", [P, NT]), sb("total", [P, NT])
        pr, tmp, oh, sel = (sb(n, [P, NT, E]) for n in ("probs", "tmp", "onehot", "selected"))
        acc = [sb(f"prefix{i}", [P, NT, E]) for i in range(2)]
        pR, pC = k.bank[0], k.bank[1]
        weights, ones_set, chain, exped, sel_ready, ranked = (sem(n) for n in (
            "weights_loaded", "ones_set", "chain", "exp_done", "selected_ready", "ranks_made"))
        shifted = sem("shifted")
        block = ctx.enter_context(nc.Block())

        @block.sync
        def _(sp):
            sp.dma_start(low[:, :], earlier).then_inc(weights, 16)
            sp.dma_start(down[:, :], countdown).then_inc(weights, 16)
            sp.wait_ge(weights, 32)

        @block.gpsimd
        def _(pool):
            pool.memset(ones[:, :], 1.0).then_inc(ones_set, 1)

        @block.scalar
        def _(act):
            act.wait_ge(shifted, 1)
            act.activation(pr[:, :, :], pr[:, :, :], ACT.Exp).then_inc(exped, 1)

        @block.tensor
        def _(pe):
            pe.wait_ge(weights, 32)
            pe.wait_ge(ones_set, 1)
            pe.wait_ge(sel_ready, 1)
            pe.matmul(pR[:, 0:NT * E], low[:, :], sel[:, :, :], start=True, stop=True)
            pe.matmul(pC[:, 0:NT * E], ones[:, :], sel[:, :, :], start=True, stop=True).then_inc(ranked, 1)

        @block.vector
        def _(dve):
            count = [0]

            def link(ins):
                ins.then_inc(chain, 1)
                count[0] += 1
                dve.wait_ge(chain, count[0])

            dve.wait_ge(weights, 32)
            link(dve.tensor_reduce(top[:, :], k.LG[:, :, :], AX, ALU.max))
            dve.tensor_tensor(pr[:, :, :], k.LG[:, :, :], spread(top[:, :], E), ALU.subtract).then_inc(shifted, 1)
            dve.wait_ge(exped, 1)
            link(dve.tensor_reduce(tot[:, :], pr[:, :, :], AX, ALU.add))
            link(dve.reciprocal(tot[:, :], tot[:, :]))
            link(dve.tensor_tensor(pr[:, :, :], pr[:, :, :], spread(tot[:, :], E), ALU.mult))
            link(dve.tensor_reduce(top[:, :], pr[:, :, :], AX, ALU.max))
            link(dve.tensor_copy(tot[:, :], top[:, :]))
            first_of(dve, link, tmp[:, :, :], sel[:, :, :], pr[:, :, :], top[:, :], down[:, :])
            link(dve.scalar_tensor_tensor(out=k.COMB[:, :, :], in0=sel[:, :, :], scalar=-2.0, in1=pr[:, :, :],
                                          op0=ALU.mult, op1=ALU.add))
            link(dve.tensor_reduce(top2[:, :], k.COMB[:, :, :], AX, ALU.max))
            link(dve.tensor_tensor(tot[:, :], tot[:, :], top2[:, :], ALU.add))
            first_of(dve, link, tmp[:, :, :], oh[:, :, :], k.COMB[:, :, :], top2[:, :], down[:, :])
            dve.tensor_tensor(sel[:, :, :], sel[:, :, :], oh[:, :, :], ALU.add).then_inc(sel_ready, 1)
            dve.wait_ge(sel_ready, 1)
            link(dve.reciprocal(tot[:, :], tot[:, :]))
            link(dve.tensor_tensor(pr[:, :, :], pr[:, :, :], spread(tot[:, :], E), ALU.mult))
            link(dve.tensor_tensor(pr[:, :, :], pr[:, :, :], sel[:, :, :], ALU.mult))
            dve.wait_ge(ranked, 1)
            link(dve.tensor_copy(acc[0][:, :, :], pC[:, 0:NT * E].rearrange("p (t e) -> p t e", e=E)))
            d, a = 1, 0
            while d < NT:
                link(dve.tensor_copy(acc[1 - a][:, 0:d, :], acc[a][:, 0:d, :]))
                link(dve.tensor_tensor(acc[1 - a][:, d:, :], acc[a][:, d:, :], acc[a][:, 0:NT - d, :], ALU.add))
                d, a = 2 * d, 1 - a
            link(dve.tensor_tensor(tmp[:, :, :], acc[a][:, :, :], pC[:, 0:NT * E].rearrange("p (t e) -> p t e", e=E),
                                   ALU.subtract))
            link(dve.tensor_tensor(tmp[:, :, :], tmp[:, :, :], pR[:, 0:NT * E].rearrange("p (t e) -> p t e", e=E),
                                   ALU.add))
            link(dve.tensor_scalar(tmp[:, :, :], tmp[:, :, :], float(CAP), None, ALU.is_lt))
            link(dve.tensor_tensor(k.COMB[:, :, 0:E], pr[:, :, :], tmp[:, :, :], ALU.mult))


def stage_experts_two(nc, k, w1d, w2d):
    E, F = 8, 256
    NF = F // P
    TB = 4
    NB = NT // TB
    with ExitStack() as ctx:
        def sb(name, shape, dt=F32):
            return ctx.enter_context(nc.sbuf_tensor("moe_" + name, shape, dt))

        sems = []

        def sem(name):
            sems.append(ctx.enter_context(nc.semaphore("moe_" + name)))
            return sems[-1]

        w1 = sb("w1", [P, E, F])
        w2 = sb("w2", [P, E, NF, D])
        ge = [sb(f"gelu{i}", [P, NF, TB * P]) for i in range(2)]
        pH = (k.bank[0:2], k.bank[2:4])
        pY = k.bank[4:6]
        weights = sem("weights_loaded")
        h_made, gelued, y_made, added, stats = (sem(n) for n in ("h_made", "gelu_done", "y_made", "added", "stats"))
        ctx.callback(clear_semaphores, nc, sems)
        block = ctx.enter_context(nc.Block())

        def blocks(eng, body):
            body(0, True, False)
            with eng.Fori(0, NB - 2) as i:
                body(i + 1, False, False)
            body(NB - 1, False, True)

        @block.sync
        def _(sp):
            sp.dma_start(w1[:, :, :], w1d).then_inc(weights, 16)
            sp.dma_start(w2[:, :, :, :], w2d).then_inc(weights, 16)
            sp.wait_ge(weights, 32)

        @block.tensor
        def _(pe):
            def h(b, e):
                n = E * b + e
                wait(pe, gelued, NF * (n - 1))
                for c in range(NF):
                    pe.matmul(pH[e % 2][c][:, :], w1[:, e, c * P:(c + 1) * P], k.LT[:, ts(b, TB), :],
                              start=True, stop=True).then_inc(h_made, 1)

            def y(n, e):
                pe.wait_ge(gelued, NF * n + NF)
                wait(pe, added, TB * (n - 1))
                for i in range(TB):
                    for c in range(NF):
                        m = pe.matmul(pY[e % 2][:, i * D:(i + 1) * D], ge[e % 2][:, c, i * P:(i + 1) * P],
                                      w2[:, e, c, :], start=(c == 0), stop=(c == NF - 1))
                m.then_inc(y_made, 1)

            def body(b, first, last):
                if first:
                    pe.wait_ge(weights, 32)
                for e in range(E):
                    h(b, e)
                    if e or not first:
                        y(E * b + e - 1, (e - 1) % E)
                if last:
                    y(E * b + E - 1, E - 1)
            blocks(pe, body)

        @block.scalar
        def _(act):
            def body(b, first, last):
                for e in range(E):
                    n = E * b + e
                    wait(act, y_made, n - 1)
                    for c in range(NF):
                        act.wait_ge(h_made, NF * n + c + 1)
                        act.activation(ge[e % 2][:, c, :], pH[e % 2][c][:, :], ACT.Gelu_apprx_tanh)\
                            .then_inc(gelued, 1)
            blocks(act, body)

        @block.vector
        def _(dve):
            def body(b, first, last):
                for e in range(E):
                    n = E * b + e
                    dve.wait_ge(y_made, n + 1)
                    for i in range(TB):
                        t = b * TB + i
                        if e:
                            dve.wait_ge(added, TB * n - TB + i + 1)
                        dve.scalar_tensor_tensor(out=k.X[:, t, :], in0=pY[e % 2][:, i * D:(i + 1) * D],
                                                 scalar=k.COMB[:, t, e:e + 1], in1=k.X[:, t, :],
                                                 op0=ALU.mult, op1=ALU.add).then_inc(added, 1)
                wait_apart(dve, added, TB * (E * b + E))
                for i in range(TB):
                    dve.bn_stats(k.BNS[:, b * TB + i, :], k.X[:, b * TB + i, :]).then_inc(stats, 1)
            blocks(dve, body)


def stage_route_one(nc, k, countdown):
    E = 8
    with ExitStack() as ctx:
        def sem(name):
            return k.semaphore("top1_" + name)

        down = ctx.enter_context(nc.sbuf_tensor("top1_countdown", [P, E], F32))
        tmp = ctx.enter_context(nc.sbuf_tensor("top1_tmp", [P, NT, E], F32))
        top = ctx.enter_context(nc.sbuf_tensor("top1_top", [P, NT], F32))
        weights, chain = sem("weights_loaded"), sem("chain")
        block = ctx.enter_context(nc.Block())

        @block.sync
        def _(sp):
            sp.dma_start(down[:, :], countdown).then_inc(weights, 16)
            sp.wait_ge(weights, 16)

        @block.vector
        def _(dve):
            count = [0]

            def link(ins):
                ins.then_inc(chain, 1)
                count[0] += 1
                dve.wait_ge(chain, count[0])

            dve.wait_ge(weights, 16)
            link(dve.tensor_reduce(top[:, :], k.LG[:, :, :], AX, ALU.max))
            first_of(dve, link, tmp[:, :, :], k.COMB[:, :, :], k.LG[:, :, :], top[:, :], down[:, :])


def stage_experts_one(nc, k, w1d, w2d, w3d):
    E, F = 9, 512
    NF = F // P
    TB = 4
    NB = NT // TB
    with ExitStack() as ctx:
        def sb(name, shape, dt=F32):
            return ctx.enter_context(nc.sbuf_tensor("glx_" + name, shape, dt))

        sems = []

        def sem(name):
            sems.append(ctx.enter_context(nc.semaphore("glx_" + name)))
            return sems[-1]

        w1 = sb("w1", [P, E, F])
        w2 = sb("w2", [P, E, F])
        w3 = sb("w3", [P, E, NF, D])
        ga = [sb(f"gelu{i}", [P, TB * P]) for i in range(2)]
        gh = [sb(f"gh{i}", [P, TB * P]) for i in range(2)]
        pA, pB, pY = k.bank[0:2], k.bank[2:4], k.bank[4:6]
        weights = sem("weights_loaded")
        a_made, b_made, gelued, gated, y_made, added = (sem(n) for n in (
            "a_made", "b_made", "gelu_done", "gated", "y_made", "added"))
        ctx.callback(clear_semaphores, nc, sems)
        block = ctx.enter_context(nc.Block())

        def blocks(eng, body):
            body(0, 0, True, False)
            body(1, 1, False, False)
            with eng.Fori(0, (NB - 4) // 2) as i:
                body(2 * i + 2, 0, False, False)
                body(2 * i + 3, 1, False, False)
            body(NB - 2, 0, False, False)
            body(NB - 1, 1, False, True)

        @block.sync
        def _(sp):
            for e in range(E):
                sp.dma_start(w1[:, e, :], w1d[e]).then_inc(weights, 16)
                sp.dma_start(w2[:, e, :], w2d[e]).then_inc(weights, 16)
                sp.dma_start(w3[:, e, :, :], w3d[e]).then_inc(weights, 16)
            sp.wait_ge(weights, 48 * E)

        @block.tensor
        def _(pe):
            def ab(b, e, c):
                n = (E * b + e) * NF + c
                wait(pe, gated, n - 1)
                pe.matmul(pA[c % 2][:, :], w1[:, e, c * P:(c + 1) * P], k.LT[:, ts(b, TB), :],
                          start=True, stop=True).then_inc(a_made, 1)
                pe.matmul(pB[c % 2][:, :], w2[:, e, c * P:(c + 1) * P], k.LT[:, ts(b, TB), :],
                          start=True, stop=True).then_inc(b_made, 1)

            def y(b, par, e, c):
                n = (E * b + e) * NF + c
                ye = E * b + e
                ys = (par + e) % 2
                pe.wait_ge(gated, n + 1)
                if c == 0:
                    wait(pe, added, TB * (ye - 1))
                for i in range(TB):
                    m = pe.matmul(pY[ys][:, i * D:(i + 1) * D], gh[c % 2][:, i * P:(i + 1) * P], w3[:, e, c, :],
                                  start=(c == 0 and i == 0), stop=(c == NF - 1 and i == TB - 1),
                                  skip_group_check=True)
                m.then_inc(y_made, 1)

            def body(b, par, first, last):
                if first:
                    pe.wait_ge(weights, 48 * E)
                for e in range(E):
                    for c in range(NF):
                        ab(b, e, c)
                        if c:
                            y(b, par, e, c - 1)
                        elif e:
                            y(b, par, e - 1, NF - 1)
                        elif not first:
                            y(b - 1, 1 - par, E - 1, NF - 1)
                if last:
                    y(b, par, E - 1, NF - 1)
            blocks(pe, body)

        @block.scalar
        def _(act):
            def body(b, par, first, last):
                for e in range(E):
                    for c in range(NF):
                        n = (E * b + e) * NF + c
                        act.wait_ge(a_made, n + 1)
                        wait(act, gated, n - 1)
                        act.activation(ga[c % 2][:, :], pA[c % 2][:, :], ACT.Gelu).then_inc(gelued, 1)
            blocks(act, body)

        @block.vector
        def _(dve):
            def gate(b, e, c):
                n = (E * b + e) * NF + c
                dve.wait_ge(gelued, n + 1)
                dve.wait_ge(b_made, n + 1)
                wait(dve, y_made, n - 1)
                dve.tensor_tensor(gh[c % 2][:, :], ga[c % 2][:, :], pB[c % 2][:, :], ALU.mult).then_inc(gated, 1)

            def add(b, par, e):
                ye = E * b + e
                dve.wait_ge(y_made, NF * ye + NF)
                for i in range(TB):
                    t = b * TB + i
                    y = pY[(par + e) % 2][:, i * D:(i + 1) * D]
                    if e:
                        dve.wait_ge(added, TB * (ye - 1) + i + 1)
                    if e < E - 1:
                        dve.scalar_tensor_tensor(out=k.X[:, t, :], in0=y, scalar=k.COMB[:, t, e:e + 1],
                                                 in1=k.X[:, t, :], op0=ALU.mult, op1=ALU.add).then_inc(added, 1)
                    else:
                        dve.tensor_tensor(k.X[:, t, :], k.X[:, t, :], y, ALU.add).then_inc(added, 1)

            def body(b, par, first, last):
                for e in range(E):
                    for c in range(NF):
                        gate(b, e, c)
                        if c == 1:
                            if e:
                                add(b, par, e - 1)
                            elif not first:
                                add(b - 1, 1 - par, E - 1)
                if last:
                    add(b, par, E - 1)
            blocks(dve, body)


def stage_cross_attention(nc, k, d):
    G, QH, HD = 4, 4, 8
    V1 = HD + 1
    PADDED = 1e9
    with ExitStack() as ctx:
        def sb(name, shape, dt=F32):
            return ctx.enter_context(nc.sbuf_tensor("xat_" + name, shape, dt))

        sems = []

        def sem(name):
            sems.append(ctx.enter_context(nc.semaphore("xat_" + name)))
            return sems[-1]

        wq, wqr, wk, wkr, wv, wo = (sb(n, [P, P]) for n in ("w_q", "w_q_rot", "w_k", "w_k_rot", "w_v", "w_out"))
        cosq, sinq = sb("cos_q", [P, P]), sb("sin_q", [P, P])
        cosk, sink = sb("cos_k", [P, J]), sb("sin_k", [P, J])
        hdiag = sb("head_of_feature", [P, QH])
        hrow = sb("head_of_row", [P, QH])
        same_q = sb("same_query", [P, S])
        nmask = sb("mask_negated", [P, J])
        cT = [sb(f"ctx_T{i}", [P, BT, JP]) for i in range(2)]
        pad = [sb(f"pad{i}", [P, BT, J], U8) for i in range(2)]
        xn = [sb(f"xn{i}", [P, D]) for i in range(2)]
        xT = [sb(f"xT{i}", [P, P]) for i in range(2)]
        qa, qc, qT = sb("q_cos", [P, P]), sb("q_sin", [P, P]), sb("q_rotated", [P, P])
        qb = [sb(f"q_blocks{i}", [P, BT, QH, S]) for i in range(2)]
        ka, kc = [sb(f"k_cos{i}", [P, J]) for i in range(2)], [sb(f"k_sin{i}", [P, J]) for i in range(2)]
        kr = sb("k_rotated", [P, J])
        kT = [sb(f"k_T{i}", [P, J]) for i in range(2)]
        keep = [sb(f"keep{i}", [P, J]) for i in range(2)]
        mb = [sb(f"mask_b{i}", [P, J]) for i in range(2)]
        mp = sb("mask_pad", [P, J])
        mk = sb("mask_kept", [P, J])
        va = [sb(f"v_ones{i}", [JC, NJ, G * QH, V1]) for i in range(2)]
        sx = [sb(f"scores{g}", [P, JP]) for g in range(G)]
        mn = [sb(f"least{g}", [P, 1]) for g in range(G)]
        pt = [sb(f"p_T{g}", [JC, NJ * P]) for g in range(G)]
        rs = sb("rsum", [P, G])
        rh = sb("rsum_head", [P, G, QH])
        om = [sb(f"o_masked{i}", [P, G * QH, HD]) for i in range(2)]
        oT = [sb(f"o_T{i}", [P, P]) for i in range(2)]
        pK, pKR, pV, pS0, pS1, pT0, pT1, pO = k.bank
        pS, pT = (pS0, pS1), (pT0, pT1)
        OC = slice(JP, JP + P)
        XC, QC, RC = slice(0, P), slice(P, 2 * P), slice(2 * P, 3 * P)

        weights, const_set, mask_ready = sem("weights_loaded"), sem("constants_set"), sem("mask_negated")
        landed = [sem("ctx_landed0"), sem("ctx_landed1")]
        normed, turned, xt_ready = sem("x_normed"), sem("x_transposed"), sem("xT_copied")
        q_made, q_cos, q_sin, q_rot, q_spread = (sem(n) for n in (
            "q_made", "q_times_cos", "q_times_sin", "q_rotated", "q_spread"))
        k_made, kr_made, v_made, v_copied = sem("k_made"), sem("kr_made"), sem("v_made"), sem("v_copied")
        k_cos, k_sin, k_sum, k_ready = (sem(n) for n in ("k_times_cos", "k_times_sin", "k_rotated", "k_ready"))
        kept, padded, mkept, mb_ready = sem("keep_ready"), sem("mask_padded"), sem("mask_kept"), sem("mask_ready")
        s_made, s_masked, s_exp = sem("scores_made"), sem("scores_masked"), sem("exp_done")
        t_made, t_copied, pv_made = sem("p_transposed"), sem("pT_copied"), sem("pv_made")
        recip, rhead, o_normed, o_turned, o_copied = (sem(n) for n in (
            "recip_done", "recip_spread", "o_normed", "o_transposed", "oT_copied"))
        y_made, added = sem("y_made"), sem("residual_chain")
        dve_waited, pool_waited = sem("dve_waited"), sem("pool_waited")
        ctx.callback(clear_semaphores, nc, sems)
        block = ctx.enter_context(nc.Block())

        loads = ((wq, "wq"), (wqr, "wq_rot"), (wk, "wk"), (wkr, "wk_rot"), (wv, "wv"), (wo, "wo"), (cosq, "cos_q"),
                 (sinq, "sin_q"), (cosk, "cos_k"), (sink, "sin_k"), (hdiag, "feature_head"), (hrow, "row_head"),
                 (same_q, "row_query"), (nmask, "mask"))
        LOADED = 16 * len(loads)

        @block.sync
        def _(sp):
            for dst, name in loads:
                sp.dma_start(dst[:, :], d["xat_" + name]).then_inc(weights, 16)

            def load(t, slot, first, last):
                wait(sp, v_made, 4 * (t - 1))
                wait(sp, padded, 4 * (t - 1))
                sp.dma_start(cT[slot][:, :, :], d["ctxT"][t]).then_inc(landed[slot], 16)
                sp.dma_start(pad[slot][:, :, :], d["xat_pad"][t].partition_broadcast(P)).then_inc(landed[slot], 16)
            steps(sp, NT, load)
            sp.wait_ge(weights, LOADED)

        def half(t, slot):
            return t // 2 if isinstance(t, int) else (t - slot) // 2

        @block.tensor
        def _(pe):
            def x_transpose(t, slot):
                pe.wait_ge(normed, t + 1)
                wait(pe, v_copied, 4 * t - 1)
                pe.transpose(pV[:, XC], xn[slot][:, :], k.ident[:, :]).then_inc(turned, 1)

            def q(t, slot):
                pe.wait_ge(xt_ready, t + 1)
                pe.matmul(pV[:, QC], wq[:, :], xT[slot][:, :], start=True, stop=True)
                pe.matmul(pV[:, RC], wqr[:, :], xT[slot][:, :], start=True, stop=True).then_inc(q_made, 1)

            def kk(t, slot, j):
                u = 4 * t + j
                if j == 0:
                    pe.wait_ge(landed[slot], 32 * (half(t, slot) + 1))
                wait(pe, k_cos, u)
                if j == 2:
                    wait(pe, o_copied, t)
                pe.matmul(pK[:, 0:J], wk[:, :], cT[slot][:, j, 0:J], start=True, stop=True).then_inc(k_made, 1)

            def kkr(t, slot, j):
                u = 4 * t + j
                wait(pe, k_sin, u)
                if j == 2:
                    wait(pe, added, 2 * (t - 1) + 1)
                pe.matmul(pKR[:, 0:J], wkr[:, :], cT[slot][:, j, 0:J], start=True, stop=True).then_inc(kr_made, 1)

            def v(t, slot, j):
                u = 4 * t + j
                wait(pe, v_copied, u)
                if j == 0:
                    pe.wait_ge(q_sin, t + 1)
                if j == 3:
                    wait(pe, q_sin, t + 2 if not isinstance(t, int) or t < NT - 1 else 0)
                for c in range(NJ):
                    m = pe.matmul(pV[0:JC, c * P:(c + 1) * P], cT[slot][:, j, c * JC:(c + 1) * JC], wv[:, :],
                                  start=True, stop=True)
                m.then_inc(v_made, 1)

            def scores(t, slot, j, g):
                u = 4 * t + j
                n = G * u + g
                pe.wait_ge(q_spread, t + 1)
                pe.wait_ge(k_ready, u + 1)
                wait(pe, s_masked, n - 1)
                r = slice(32 * g, 32 * g + 32)
                pe.matmul(pS[g % 2][:, 0:J], qb[slot][r, j, :, :], kT[j % 2][r, :], start=True, stop=True)\
                    .then_inc(s_made, 1)

            def p_transpose(n, g):
                pe.wait_ge(s_exp, n + 1)
                wait(pe, t_copied, n - 1)
                for c in range(NJ):
                    m = pe.transpose(pT[g % 2][0:JC, c * P:(c + 1) * P], sx[g][:, c * JC:(c + 1) * JC], k.ident[:, :])
                m.then_inc(t_made, 1)

            def pv(n, j, g):
                pe.wait_ge(t_copied, n + 1)
                if g == 0:
                    wait(pe, o_normed, (n - g) // G if isinstance(n, int) else n // G)
                for c in range(NJ):
                    m = pe.matmul(pO[:, g * QH * V1:(g + 1) * QH * V1], pt[g][:, c * P:(c + 1) * P],
                                  va[j % 2][:, c, g * QH:(g + 1) * QH, :], start=(c == 0), stop=(c == NJ - 1))
                m.then_inc(pv_made, 1)

            def o_transpose(u, j, ahead):
                pe.wait_ge(o_normed, u + 1)
                wait(pe, k_cos, u + 1 + ahead)
                o = JP + j * S
                pe.matmul(pK[:, o:o + S], om[j % 2][:, :, :], same_q[:, :], start=True, stop=True).then_inc(o_turned, 1)

            def y(t, slot, ksin):
                pe.wait_ge(o_copied, t + 1)
                pe.wait_ge(k_sin, ksin)
                pe.matmul(pKR[:, OC], oT[slot][:, :], wo[:, :], start=True, stop=True).then_inc(y_made, 1)

            def body(t, slot, first, last):
                if first:
                    pe.wait_ge(weights, LOADED)
                    pe.wait_ge(const_set, 6)
                    x_transpose(t, slot)
                    q(t, slot)
                    kk(t, slot, 0)
                    kkr(t, slot, 0)
                    v(t, slot, 0)
                for j in range(BT):
                    u = BT * t + j
                    nxt = (t, slot, j + 1) if j < BT - 1 else (t + 1, 1 - slot, 0)
                    ahead = not (last and j == BT - 1)
                    start = first and j == 0
                    for g in range(G):
                        n = G * u + g
                        scores(t, slot, j, g)
                        if not (start and g < 2):
                            p_transpose(n - 2, (g - 2) % G)
                        if not (start and g < 3):
                            pv(n - 3, j if g == 3 else (j - 1) % BT, (g - 3) % G)
                        if g == 0 and j == 1 and not first:
                            y(t - 1, 1 - slot, u + 1)
                        if g == 0 and j == 2 and not last:
                            x_transpose(t + 1, 1 - slot)
                        if g == 1 and ahead:
                            kk(*nxt)
                        if g == 2 and ahead:
                            kkr(*nxt)
                        if g == 2 and j == 2 and not last:
                            q(t + 1, 1 - slot)
                        if g == 3 and ahead:
                            v(*nxt)
                        if g == 3 and not start:
                            o_transpose(u - 1, (j - 1) % BT, 2 if ahead else 1)
                if last:
                    for g in range(2, G):
                        p_transpose(G * u + g, g)
                    for g in range(1, G):
                        pv(G * u + g, j, g)
                    o_transpose(u, j, 0)
                    y(t, slot, BT * NT)
            steps(pe, NT, body)

        @block.scalar
        def _(act):
            def x_copy(t, slot):
                act.wait_ge(turned, t + 1)
                wait(act, q_made, t - 1)
                act.activation(xT[slot][:, :], pV[:, XC], ACT.Copy).then_inc(xt_ready, 1)

            def v_copy(u, j):
                act.wait_ge(v_made, u + 1)
                wait(act, pv_made, G * (u - 1))
                act.activation(va[j % 2][:, :, :, 0:HD],
                               pV[0:JC, 0:NJ * P].rearrange("p (c h d) -> p c h d", c=NJ, d=HD),
                               ACT.Copy).then_inc(v_copied, 1)

            def exp(n, g):
                act.wait_ge(s_masked, n + 1)
                act.activation(sx[g][:, 0:J], sx[g][:, 0:J], ACT.Exp, bias=mn[g][:, 0:1], scale=-1.0)\
                    .then_inc(s_exp, 1)

            def t_copy(n, g):
                act.wait_ge(t_made, n + 1)
                wait(act, pv_made, n - 3)
                act.activation(pt[g][:, :], pT[g % 2][0:JC, 0:NJ * P], ACT.Copy).then_inc(t_copied, 1)

            def o_copy(t, slot):
                act.wait_ge(o_turned, BT * t + BT)
                wait(act, y_made, t - 1)
                act.activation(oT[slot][:, :], pK[:, OC], ACT.Copy).then_inc(o_copied, 1)

            def body(t, slot, first, last):
                if first:
                    act.wait_ge(const_set, 6)
                    x_copy(t, slot)
                    v_copy(0, 0)
                for j in range(BT):
                    u = BT * t + j
                    start = first and j == 0
                    for g in range(G):
                        n = G * u + g
                        if not (start and g < 1):
                            exp(n - 1, (g - 1) % G)
                        if not (start and g < 2):
                            t_copy(n - 2, (g - 2) % G)
                        if g == 0 and j == 1 and not first:
                            o_copy(t - 1, 1 - slot)
                        if g == 1 and j == 2 and not last:
                            x_copy(t + 1, 1 - slot)
                        if g == 3 and not (last and j == BT - 1):
                            v_copy(u + 1, (j + 1) % BT)
                if last:
                    exp(G * u + 3, 3)
                    t_copy(G * u + 2, 2)
                    t_copy(G * u + 3, 3)
                    o_copy(t, slot)
            steps(act, NT, body)

        @block.gpsimd
        def _(pool):
            def prepare(t, slot, j):
                u = BT * t + j
                if j == 0:
                    pool.wait_ge(landed[slot], 32 * (half(t, slot) + 1))
                    pool.sem_inc(pool_waited, 1)
                pool.tensor_scalar(keep[j % 2][:, :], pad[slot][:, j, :], -1.0, 1.0, ALU.mult, ALU.add)\
                    .then_inc(kept, 1)
                pool.tensor_scalar(mp[:, :], pad[slot][:, j, :], PADDED, 0.0, ALU.mult, ALU.add).then_inc(padded, 1)
                pool.wait_ge(kept, u + 1)
                pool.tensor_tensor(mk[:, :], keep[j % 2][:, :], nmask[:, :], ALU.mult).then_inc(mkept, 1)
                pool.wait_ge(mkept, u + 1)
                pool.wait_ge(padded, u + 1)
                wait(pool, s_masked, G * (u - 1))
                pool.tensor_tensor(mb[j % 2][:, :], mk[:, :], mp[:, :], ALU.add).then_inc(mb_ready, 1)
                pool.wait_ge(k_sin, u + 1)
                pool.tensor_tensor(kr[:, :], ka[j % 2][:, :], kc[j % 2][:, :], ALU.add).then_inc(k_sum, 1)
                pool.wait_ge(k_sum, u + 1)
                wait(pool, s_made, G * (u - 1))
                pool.tensor_tensor(kT[j % 2][:, :], kr[:, :], keep[j % 2][:, :], ALU.mult).then_inc(k_ready, 1)

            def body(t, slot, first, last):
                if first:
                    for i in range(2):
                        pool.memset(va[i][:, :, :, HD:V1], 1.0).then_inc(const_set, 1)
                    for g in range(G):
                        pool.memset(sx[g][:, J:JP], 0.0).then_inc(const_set, 1)
                    pool.wait_ge(mask_ready, 1)
                    prepare(t, slot, 0)
                for j in range(BT):
                    if j < BT - 1:
                        prepare(t, slot, j + 1)
                    elif not last:
                        prepare(t + 1, 1 - slot, 0)
            steps(pool, NT, body)

        @block.vector
        def _(dve):
            def norm(t, slot):
                wait(dve, turned, t - 1)
                dve.tensor_scalar(xn[slot][:, :], k.X[:, t, :], k.MV[:, t, 0:1], k.RSTD[:, ts(t, 1)],
                                  ALU.subtract, ALU.mult).then_inc(normed, 1)

            def rotate_q(t, slot):
                dve.wait_ge(q_made, t + 1)
                dve.tensor_tensor(qa[:, :], pV[:, QC], cosq[:, :], ALU.mult).then_inc(q_cos, 1)
                dve.tensor_tensor(qc[:, :], pV[:, RC], sinq[:, :], ALU.mult).then_inc(q_sin, 1)
                dve.wait_ge(q_cos, t + 1)
                dve.wait_ge(q_sin, t + 1)
                dve.tensor_tensor(qT[:, :], qa[:, :], qc[:, :], ALU.add).then_inc(q_rot, 1)
                dve.wait_ge(q_rot, t + 1)
                wait(dve, s_made, BT * G * (t - 1))
                for j in range(BT):
                    m = dve.tensor_tensor(qb[slot][:, j, :, :],
                                          qT[:, j * S:(j + 1) * S].unsqueeze(1).broadcast_to([P, QH, S]),
                                          spread(hdiag[:, :], S), ALU.mult)
                m.then_inc(q_spread, 1)

            def rotate_k(u, j):
                dve.wait_ge(k_made, u + 1)
                wait(dve, k_sum, u - 1)
                dve.tensor_tensor(ka[j % 2][:, :], pK[:, 0:J], cosk[:, :], ALU.mult).then_inc(k_cos, 1)
                dve.wait_ge(kr_made, u + 1)
                dve.tensor_tensor(kc[j % 2][:, :], pKR[:, 0:J], sink[:, :], ALU.mult).then_inc(k_sin, 1)

            def mask(n, u, j, g):
                dve.wait_ge(s_made, n + 1)
                dve.wait_ge(mb_ready, u + 1)
                wait(dve, t_made, n - 3)
                dve.sem_inc(dve_waited, 1)
                dve.tensor_tensor_reduce(sx[g][:, 0:J], pS[g % 2][:, 0:J], mb[j % 2][:, :], 1.0, BIG,
                                         ALU.add, ALU.min, mn[g][:, 0:1]).then_inc(s_masked, 1)

            def o_norm(u, j):
                dve.wait_ge(pv_made, G * u + G)
                o4 = pO[:, 0:G * QH * V1].rearrange("p (g x) -> p g x", x=QH * V1)
                dve.reciprocal(rs[:, :], o4[:, :, HD]).then_inc(recip, 1)
                dve.wait_ge(recip, u + 1)
                dve.tensor_tensor(rh[:, :, :], spread(rs[:, :], QH), hrow[:, :].unsqueeze(1).broadcast_to([P, G, QH]),
                                  ALU.mult).then_inc(rhead, 1)
                dve.wait_ge(rhead, u + 1)
                wait(dve, o_turned, u - 1)
                dve.tensor_tensor(om[j % 2][:, :, :],
                                  pO[:, 0:G * QH * V1].rearrange("p (h x) -> p h x", x=V1)[:, :, 0:HD],
                                  spread(rh[:, :, :].rearrange("p g h -> p (g h)"), HD), ALU.mult).then_inc(o_normed, 1)

            def add(t):
                dve.wait_ge(y_made, t + 1)
                residual_tile(dve, k, t, pKR[:, OC], added, 2 * t)

            def body(t, slot, first, last):
                if first:
                    dve.wait_ge(weights, LOADED)
                    norm(t, slot)
                    dve.tensor_scalar(nmask[:, :], nmask[:, :], -1.0, None, ALU.mult).then_inc(mask_ready, 1)
                    rotate_q(t, slot)
                    rotate_k(0, 0)
                for j in range(BT):
                    u = BT * t + j
                    start = first and j == 0
                    for g in range(G):
                        mask(G * u + g, u, j, g)
                        if g == 1 and j == 1 and not last:
                            norm(t + 1, 1 - slot)
                        if g == 1 and j == 1 and not first:
                            add(t - 1)
                        if g == 2 and not (last and j == BT - 1):
                            rotate_k(u + 1, (j + 1) % BT)
                        if g == 2 and not start:
                            o_norm(u - 1, (j - 1) % BT)
                        if g == 2 and j == 2 and not last:
                            rotate_q(t + 1, 1 - slot)
                if last:
                    o_norm(u, j)
                    add(t)
            steps(dve, NT, body)


STAGES = (1, 2, 3, 4, 5, 6)


def build(nc, a, out):
    with ExitStack() as ctx:
        k = Core(nc, ctx)

        def sb(name, shape, dt=F32):
            return ctx.enter_context(nc.sbuf_tensor(name, shape, dt))

        k.bank = [ctx.enter_context(nc.psum_tensor(f"bank{i}", [P, 512], F32)) for i in range(8)]
        k.X = sb("X", [P, NT, D])
        k.MV = sb("mean_var", [P, NT, 2])
        k.RSTD = sb("rstd", [P, NT])
        k.SD = sb("std", [P, NT])
        k.BNS = sb("bn_stats", [P, NT, 6])
        k.eps = sb("eps", [P, 2])
        k.MS = sb("mean_square", [P, NT])
        k.ident = sb("ident", [P, P])
        k.LG = sb("logits", [P, NT, 8])
        k.COMB = sb("expert_shares", [P, NT, 8])
        load_phase(nc, k, a["x"], [(k.ident[:, :], a["ident"])])
        if 1 in STAGES:
            deviation_phase(nc, k, "ln1")
            stage_ctx_glu(nc, k, a["ctxT"], a["ctxN"])
        if 2 in STAGES:
            deviation_phase(nc, k, "ln2")
            stage_linear_attention(nc, k, a["lin_wqkv"], a["lin_wout"], a["lin_bout"], a["same_batch"])
        if 3 in STAGES:
            with ExitStack() as moe:
                k.HID = moe.enter_context(nc.sbuf_tensor("hidden", [P, NT, D], F32))
                k.LT = moe.enter_context(nc.sbuf_tensor("ln_T", [P, NT, P], F32))
                k.AT = moe.enter_context(nc.sbuf_tensor("attn_T", [P, NT, P], F32))
                deviation_phase(nc, k, "ln3")
                stage_hidden(nc, k)
                deviation_phase(nc, k, "ln3a")
                stage_norm_transpose(nc, k, "ln3b", k.HID, a["moe_ln1"])
                stage_batch_attention(nc, k, a["bat_wq"], a["bat_wk"], a["bat_wv"], a["bat_head_diag"],
                                      a["bat_causal"])
                stage_projection(nc, k, a["bat_wproj"])
                deviation_phase(nc, k, "ln3c")
                stage_norm_transpose(nc, k, "ln3d", k.HID, a["moe_ln2"], a["moe_router"])
                stage_route_two(nc, k, a["earlier"], a["countdown"])
                stage_experts_two(nc, k, a["moe_w1"], a["moe_w2"])
        if 4 in STAGES:
            deviation_phase(nc, k, "ln4")
            stage_cross_attention(nc, k, a)
        if 5 in STAGES:
            deviation_phase(nc, k, "ln5", rms=True)
            stage_clamped_attention(nc, k, a["gqa_wq"], a["gqa_wkv"], a["gqa_wout"], a["gqa_gamma"],
                                    a["gqa_normw"], a["causal"])
        if 6 in STAGES:
            with ExitStack() as moe:
                k.LT = moe.enter_context(nc.sbuf_tensor("ln6_T", [P, NT, P], F32))
                deviation_phase(nc, k, "ln6")
                stage_norm_transpose(nc, k, "ln6a", k.X, None, a["glx_router"])
                stage_route_one(nc, k, a["countdown"])
                stage_experts_one(nc, k, a["glx_w1"], a["glx_w2"], a["glx_w3"])
        store_phase(nc, k, out)


def layouts(i):
    g = {n: np.ascontiguousarray(v) for n, v in i.items()}
    o = {"x": g["x"]}
    o["ident"] = np.eye(P, dtype=np.float32)
    ctx = np.zeros((B, JP, D), np.float32)
    ctx[:, :J] = g["ctx_1024"]
    o["ctxT"] = ctx.reshape(NT, BT, JP, D).transpose(0, 3, 1, 2)
    o["ctxN"] = ctx.reshape(NT, BT, NJ, JC, D).transpose(0, 3, 1, 2, 4)
    row = np.arange(P)
    o["same_batch"] = (row[:, None] // S == row[None] // S).astype(np.float32)
    o["lin_wqkv"] = g["L0_attn_w_qkv"].reshape(D, 3, 2, 512)
    o["lin_wout"] = g["L0_attn_w_out"].reshape(8, P, D).transpose(1, 0, 2)
    o["lin_bout"] = g["L0_attn_b_out"].reshape(1, D)
    o["causal"] = ((row[:, None] // S == row[None] // S) & (row[:, None] <= row[None])).astype(np.float32)
    order = [half * 8 + 2 * (2 * (c // 2) + r) + c % 2 for half in range(2) for c in range(4) for r in range(2)]
    o["gqa_wq"] = g["L1_attn_Wq"].reshape(D, 16, 64)[:, order].reshape(D, 2, 512)
    o["gqa_wkv"] = g["L1_attn_Wkv"].reshape(D, 2, 2, 256).transpose(0, 2, 1, 3).reshape(D, 2, 512)
    o["gqa_wout"] = g["L1_attn_Wout"].reshape(4, P, D).transpose(1, 0, 2)
    qg = g["L1_attn_q_gamma"][order].reshape(2, 4, P)
    kg = g["L1_attn_k_gamma"].reshape(2, 2, P)
    o["gqa_gamma"] = np.concatenate([qg, kg], 1).transpose(2, 0, 1).reshape(P, 12)
    o["gqa_normw"] = g["L1_attn_norm_w"].reshape(D, 1)
    qkv = g["L0_ffn_qkv_weight"].reshape(4, 48, D)
    o["bat_wq"] = qkv[:, 0:32].reshape(P, D).T
    o["bat_wk"] = np.tile(qkv[:, 32:40], (1, 4, 1)).reshape(P, D).T
    o["bat_wv"] = qkv[:, 40:48].reshape(32, D).T
    o["bat_wproj"] = g["L0_ffn_proj_weight"].T
    o["bat_head_diag"] = ((row[:, None] % 32) // 8 == np.arange(4)[None]).astype(np.float32)
    o["bat_causal"] = np.where(row[:, None] >= row[None], 0.0, -1e30).astype(np.float32)
    o["moe_ln1"] = np.stack([g["L0_ffn_ln1_weight"], g["L0_ffn_ln1_bias"]], 1)
    o["moe_ln2"] = np.stack([g["L0_ffn_ln2_weight"], g["L0_ffn_ln2_bias"]], 1)
    o["moe_router"] = g["L0_ffn_router_weight"]
    o["earlier"] = (row[:, None] < row[None]).astype(np.float32)
    o["countdown"] = np.tile(np.arange(8, 0, -1, dtype=np.float32), (P, 1))
    o["moe_w1"] = g["L0_ffn_moe_w1"].transpose(1, 0, 2)
    o["moe_w2"] = g["L0_ffn_moe_w2"].reshape(8, 2, P, D).transpose(2, 0, 1, 3)
    o["glx_router"] = g["L1_ffn_Wg"]
    o["glx_w1"] = np.concatenate([g["L1_ffn_W1"], g["L1_ffn_w1s"][None]])
    o["glx_w2"] = np.concatenate([g["L1_ffn_W2"], g["L1_ffn_w2s"][None]])
    w3 = np.concatenate([g["L1_ffn_W3"], g["L1_ffn_w3s"][None]])
    o["glx_w3"] = w3.reshape(9, 4, P, D).transpose(0, 2, 1, 3)
    swap = np.arange(P) ^ 1
    for w in ("q", "k"):
        m = g["L1_xattn_W" + w].T
        o["xat_w" + w], o["xat_w" + w + "_rot"] = m, m[:, swap]
    o["xat_wv"], o["xat_wo"] = g["L1_xattn_Wv"].T, g["L1_xattn_Wo"].T
    inv = (1.0 / 10000.0 ** (np.arange(0, 8, 2, dtype=np.float32) / 8)).astype(np.float32)
    angle = np.arange(J, dtype=np.float32)[:, None] * np.concatenate([inv, inv])[None]
    sign = np.where(np.arange(8) % 2, 1.0, -1.0)
    cos, sin = np.tile(np.cos(angle).T, (16, 1)), np.tile((np.sin(angle) * sign).T, (16, 1))
    o["xat_cos_k"], o["xat_sin_k"] = cos.astype(np.float32), sin.astype(np.float32)
    for n, v in (("xat_cos_q", cos), ("xat_sin_q", sin)):
        o[n] = (-np.tile(v[:, :S], (1, BT)) / np.sqrt(8)).astype(np.float32)
    o["xat_feature_head"] = o["bat_head_diag"]
    o["xat_row_head"] = (row[:, None] // 32 == np.arange(4)[None]).astype(np.float32)
    o["xat_row_query"] = (row[:, None] % 32 == np.arange(32)[None]).astype(np.float32)
    o["xat_mask"] = np.tile(g["mask_1x1xSxS2_fk0"].reshape(S, J), (4, 1))
    o["xat_pad"] = g["mask_BxS2_bk0"].reshape(NT, BT * J)
    return {n: np.ascontiguousarray(v) for n, v in o.items()}


def kernel(**inputs):
    import concourse.bacc as _bacc
    from concourse import mybir as _mybir
    from concourse.bass_utils import run_bass_kernel_spmd as _run

    nc = _bacc.Bacc("TRN2", target_bir_lowering=False, num_devices=1)
    arrays, a = {}, {}
    for name, v in layouts(inputs).items():
        arrays[f"in_{name}"] = v
        a[name] = nc.dram_tensor(f"in_{name}", v.shape, _mybir.dt.from_np(v.dtype), kind="ExternalInput").ap()
    out = nc.dram_tensor("out_0", (B, S, D), F32, kind="ExternalOutput").ap()
    build(nc, a, out)
    r = _run(nc, [arrays], core_ids=[0])
    return r.results[0]["out_0"]
```
